# Optimizing a Trainium2 kernel written in Bass

```python
import numpy as np
import jax
import jax.numpy as jnp

def _softmax(x, axis=-1):
    return jax.nn.softmax(x, axis=axis)

def _gelu(x):
    return jax.nn.gelu(x, approximate=True)

def _silu(x):
    return jax.nn.silu(x)

def _sigmoid(x):
    return jax.nn.sigmoid(x)

def _layernorm(x, axis=-1, eps=1e-05):
    m = jnp.mean(x, axis=axis, keepdims=True)
    v = jnp.var(x, axis=axis, keepdims=True)
    return (x - m) / jnp.sqrt(v + eps)

def _scatter_add(tgt, idx, src, axis=0):
    return tgt.at[idx].add(src)

def _segment_sum(src, seg, n):
    return jax.ops.segment_sum(src, seg, n)
kernel_name = 'mk_seq_postln_d1_jaxref_r8_51399b'

def setup_inputs(seed: int=0):
    np.random.seed(seed)
    _w = jnp.asarray

    def _L0_attn_setup():
        import jax, jax.numpy as jnp
        import numpy as np
        import math
        B, S, D_IN, D_KQ, D_OUT = (4, 256, 128, 128, 128)
        key = jax.random.key(seed)
        ks = jax.random.split(key, 7)
        sc = 0.02
        return {'x': jax.random.normal(ks[0], (B, S, D_IN), jnp.float32), 'Wq': jax.random.normal(ks[1], (D_KQ, D_IN), jnp.float32) * sc, 'bq': jax.random.normal(ks[2], (D_KQ,), jnp.float32) * sc, 'Wk': jax.random.normal(ks[3], (D_KQ, D_IN), jnp.float32) * sc, 'bk': jax.random.normal(ks[4], (D_KQ,), jnp.float32) * sc, 'Wv': jax.random.normal(ks[5], (D_OUT, D_IN), jnp.float32) * sc, 'bv': jax.random.normal(ks[6], (D_OUT,), jnp.float32) * sc}
    _L0_attn_in = _L0_attn_setup()

    def _L0_ffn_setup():
        import jax, jax.numpy as jnp
        import numpy as np
        DIM = 128
        INTER = 128
        N_EXPERTS = 8
        TOPK = 2
        N_SHARED = 2
        key = jax.random.key(seed)
        ks = jax.random.split(key, 10)
        s = 0.02
        return {'x': jax.random.normal(ks[0], (4, 256, DIM), dtype=jnp.float32), 'gate_w': jax.random.normal(ks[1], (N_EXPERTS, DIM), dtype=jnp.float32) * s, 'gate_bias': jax.random.normal(ks[2], (N_EXPERTS,), dtype=jnp.float32) * s, 'w1': jax.random.normal(ks[3], (N_EXPERTS, INTER, DIM), dtype=jnp.float32) * s, 'w3': jax.random.normal(ks[4], (N_EXPERTS, INTER, DIM), dtype=jnp.float32) * s, 'w2': jax.random.normal(ks[5], (N_EXPERTS, DIM, INTER), dtype=jnp.float32) * s, 'sw1': jax.random.normal(ks[6], (N_SHARED * INTER, DIM), dtype=jnp.float32) * s, 'sw3': jax.random.normal(ks[7], (N_SHARED * INTER, DIM), dtype=jnp.float32) * s, 'sw2': jax.random.normal(ks[8], (DIM, N_SHARED * INTER), dtype=jnp.float32) * s}
    _L0_ffn_in = _L0_ffn_setup()
    _d = {'L0_attn_x': _L0_attn_in['x'], 'L0_attn_Wq': _L0_attn_in['Wq'], 'L0_attn_bq': _L0_attn_in['bq'], 'L0_attn_Wk': _L0_attn_in['Wk'], 'L0_attn_bk': _L0_attn_in['bk'], 'L0_attn_Wv': _L0_attn_in['Wv'], 'L0_attn_bv': _L0_attn_in['bv'], 'L0_ffn_gate_w': _L0_ffn_in['gate_w'], 'L0_ffn_gate_bias': _L0_ffn_in['gate_bias'], 'L0_ffn_w1': _L0_ffn_in['w1'], 'L0_ffn_w3': _L0_ffn_in['w3'], 'L0_ffn_w2': _L0_ffn_in['w2'], 'L0_ffn_sw1': _L0_ffn_in['sw1'], 'L0_ffn_sw3': _L0_ffn_in['sw3'], 'L0_ffn_sw2': _L0_ffn_in['sw2']}
    _x0 = _d['L0_attn_x']
    _d['L0_attn_x'] = jax.random.normal(jax.random.fold_in(jax.random.key(seed), 1), (2, 1024, 128), dtype=_x0.dtype)
    del _x0
    return _d

def reference(L0_attn_x, L0_attn_Wq, L0_attn_bq, L0_attn_Wk, L0_attn_bk, L0_attn_Wv, L0_attn_bv, L0_ffn_gate_w, L0_ffn_gate_bias, L0_ffn_w1, L0_ffn_w3, L0_ffn_w2, L0_ffn_sw1, L0_ffn_sw3, L0_ffn_sw2):

    def _L0_attn_ref(x, Wq, bq, Wk, bk, Wv, bv):
        import jax, jax.numpy as jnp
        import numpy as np
        import math
        B, S, D_IN, D_KQ, D_OUT = (4, 256, 128, 128, 128)
        Q = jnp.einsum('bsd,kd->bsk', x, Wq) + bq
        K = jnp.einsum('bsd,kd->bsk', x, Wk) + bk
        V = jnp.einsum('bsd,od->bso', x, Wv) + bv
        scale = 1.0 / math.sqrt(D_KQ)
        attn = jnp.einsum('bqk,bsk->bqs', Q, K) * scale
        s = attn.shape[-1]
        causal = jnp.tril(jnp.ones((s, s), dtype=bool))
        attn = jnp.where(causal[None, :, :], attn, -jnp.inf)
        attn = jax.nn.softmax(attn, axis=-1)
        Z = jnp.einsum('bqs,bso->bqo', attn, V)
        return Z

    def _L0_ffn_ref(x, gate_w, gate_bias, w1, w3, w2, sw1, sw3, sw2):
        import jax, jax.numpy as jnp
        import numpy as np
        DIM = 128
        INTER = 128
        N_EXPERTS = 8
        TOPK = 2
        N_SHARED = 2
        shape = x.shape
        xt = x.reshape(-1, shape[-1])
        scores = jax.nn.softmax((xt @ gate_w.T).astype(jnp.float32), axis=-1)
        _, idx = jax.lax.top_k(scores + gate_bias, TOPK)
        weights = jnp.take_along_axis(scores, idx, axis=1).astype(x.dtype)
        y = jnp.zeros_like(xt)
        for e in range(N_EXPERTS):
            gate_e = jnp.sum(jnp.where(idx == e, weights, 0.0), axis=1)
            h = jax.nn.silu(xt @ w1[e].T) * (xt @ w3[e].T)
            y = y + gate_e[:, None] * (h @ w2[e].T)
        z = jax.nn.silu(xt @ sw1.T) * (xt @ sw3.T) @ sw2.T
        return (y + z).reshape(shape)
    x = L0_attn_x
    x = _layernorm(x + _L0_attn_ref(x, L0_attn_Wq, L0_attn_bq, L0_attn_Wk, L0_attn_bk, L0_attn_Wv, L0_attn_bv), axis=-1)
    x = _layernorm(x + _L0_ffn_ref(x, L0_ffn_gate_w, L0_ffn_gate_bias, L0_ffn_w1, L0_ffn_w3, L0_ffn_w2, L0_ffn_sw1, L0_ffn_sw3, L0_ffn_sw2), axis=-1)
    return x

_drawn_inputs = setup_inputs


def setup_inputs(seed=0):
    import zlib

    import numpy as np

    out = dict(_drawn_inputs(seed))
    spreads = {}
    factors = {'L0_attn_Wq': 8.0,
     'L0_attn_bq': 8.0,
     'L0_attn_Wk': 8.0,
     'L0_attn_bk': 8.0,
     'L0_attn_Wv': 2.923,
     'L0_ffn_gate_w': 8.0,
     'L0_ffn_gate_bias': 8.0,
     'L0_ffn_w1': 8.0,
     'L0_ffn_w3': 8.0,
     'L0_ffn_w2': 8.0,
     'L0_ffn_sw1': 6.944,
     'L0_ffn_sw3': 6.895,
     'L0_ffn_sw2': 6.903}
    for name, (base, spread) in spreads.items():
        noise = np.random.default_rng([zlib.crc32(name.encode()), seed]).standard_normal(out[name].shape)
        drawn = base * np.exp(spread * noise) if base else spread * noise
        out[name] = jnp.asarray(drawn.astype(out[name].dtype))
    for name, factor in factors.items():
        out[name] = (out[name] * factor).astype(out[name].dtype)
    return out
```

```python
import concourse.bass as bass
from concourse import mybir
from contextlib import ExitStack


def attention_moe_block(nc, x, xT_in, w_att, b_qk, b_v, gate_wT, gate_b, w1T_in, w3T_in, w2T_in, out):
    f32, f32r, bf16 = mybir.dt.float32, mybir.dt.float32r, mybir.dt.bfloat16
    u32, i32 = mybir.dt.uint32, mybir.dt.int32
    ALU, ACT, AX = mybir.AluOpType, mybir.ActivationFunctionType, mybir.AxisListType

    B, S, D = x.shape
    P = 128
    C = 512
    CT = C // P
    ST = S // P
    NCH = B * S // C
    E = gate_wT.shape[1]
    NE = w1T_in.shape[1] // P
    SH = NE - E
    SCALE = float(D) ** -0.5
    EPS = 1e-5
    MASKED = -1e30
    EULER = 2.718281828459045
    assert D == P and S == 2 * C

    GROUPS = [[(j0, min(j0 + CT, i + 1)) for j0 in range(0, i + 1, CT)] for i in range(ST)]
    G0 = [sum(len(g) for g in GROUPS[:i]) for i in range(ST + 1)]
    GPS = G0[ST]

    def by_act(g):
        return g % 2 == 0

    def groups_of(act, upto):
        return sum(by_act(g % GPS) == act for g in range(upto))

    gates_dram = nc.dram_tensor("gates_scratch", (NCH, CT * E, P), f32, kind="Internal").ap()

    with ExitStack() as ctx:
        def sb(name, shape, dt=f32):
            return ctx.enter_context(nc.sbuf_tensor(name, shape, dt))

        def sem(name):
            return ctx.enter_context(nc.semaphore(name))

        ident = sb("ident", [P, P])
        ident16 = sb("ident16", [P, P], bf16)
        mask16 = sb("mask16", [P, P], bf16)
        expert_no = sb("expert_no", [P, CT, E], i32)
        euler = sb("euler", [P, CT, E])
        minus_half = sb("minus_half", [P, CT])
        watt = sb("watt", [P, 3 * P])
        bqk = sb("bqk", [P, 2])
        bv = sb("bv", [P, D])
        gw = sb("gw", [P, E])
        gw_hi = sb("gw_hi", [P, E], f32r)
        gw_lo = sb("gw_lo", [P, E], f32r)
        gb = sb("gb", [P, E])
        wf = [sb(f"w{n}", [P, NE * P]) for n in "132"]
        wf_hi = [sb(f"w{n}_hi", [P, NE * P], f32r) for n in "132"]
        wf_lo = [sb(f"w{n}_lo", [P, NE * P], f32r) for n in "132"]
        xs = sb("xs", [P, B * ST, D])
        xT = sb("xT", [P, B * S])
        kT = sb("kT", [P, S])
        qT = sb("qT", [P, S])
        v = sb("v", [P, ST, D])
        negmax = sb("negmax", [P, B * ST])
        rowsum = sb("rowsum", [P, B * ST])
        rinv = sb("rinv", [P, B * ST])
        probs = sb("probs", [P, 2, S])
        pT = sb("pT", [P, CT + ST, C])
        zT = sb("zT", [P, 2, C])
        y1 = sb("y1", [P, B * ST, D])
        x1 = sb("x1", [P, B * ST, D])
        x1T_hi = sb("x1T_hi", [P, 2, C], f32r)
        x1T_lo = sb("x1T_lo", [P, 2, C], f32r)
        stats = sb("stats", [P, 2, CT, 6])
        mv1 = sb("mv1", [P, B * ST, 2])
        mv2 = sb("mv2", [P, B * ST, 2])
        ve1 = sb("ve1", [P, B * ST])
        ve2 = sb("ve2", [P, B * ST])
        rstd1 = sb("rstd1", [P, B * ST])
        rstd2 = sb("rstd2", [P, B * ST])
        lmax = sb("lmax", [P, CT])
        cent = sb("cent", [P, NCH, CT, E])
        expo = sb("expo", [P, NCH, CT, E])
        esum = sb("esum", [P, CT])
        einv = sb("einv", [P, CT])
        score = sb("score", [P, CT, E])
        biased = sb("biased", [P, CT, E])
        top = sb("top", [P, CT, 8])
        topi = sb("topi", [P, CT, 8], u32)
        is0 = sb("is0", [P, CT, E])
        is1 = sb("is1", [P, CT, E])
        gates = sb("gates", [P, NCH, P])
        gatesT = sb("gatesT", [P, NCH, P])
        gspread = sb("gspread", [P, 2, CT, E, P])
        silu = sb("silu", [P, 3, C])
        h = sb("h", [P, 3, C])
        h_hi = sb("h_hi", [P, 3, C], f32r)
        h_lo = sb("h_lo", [P, 3, C], f32r)
        yT = sb("yT", [P, 2, C])
        y2 = y1
        o = y2

        ps_s = ctx.enter_context(nc.psum_tensor("ps_s", [P, 2, S], f32))
        ps_t = ctx.enter_context(nc.psum_tensor("ps_t", [P, 2, C], f32))
        ps_z = ctx.enter_context(nc.psum_tensor("ps_z", [P, C], f32))
        ps_m = ctx.enter_context(nc.psum_tensor("ps_m", [P, C], f32))
        ps_y = [ps_z, ps_m]

        consts_ready = sem("consts_ready")
        pool_step = sem("pool_step")
        ld_xT = [sem(f"ld_xT{b}") for b in range(B)]
        ld_watt, ld_bias, ld_x = sem("ld_watt"), sem("ld_bias"), sem("ld_x")
        ld_wf = [sem(f"ld_w{n}") for n in "132"]
        watt_ready, w_hi_ready, w_lo_ready = sem("watt_ready"), sem("w_hi_ready"), sem("w_lo_ready")
        proj_ready, kq_ready, v_ready = sem("proj_ready"), sem("kq_ready"), sem("v_ready")
        scores_ready, negmax_ready, probs_ready = sem("scores_ready"), sem("negmax_ready"), sem("probs_ready")
        pT_made, pT_by_act, pT_by_dve = sem("pT_made"), sem("pT_by_act"), sem("pT_by_dve")
        zT_made, zT_ready, z_made = sem("zT_made"), sem("zT_ready"), sem("z_made")
        var1_ready, rstd1_ready, x1_ready = sem("var1_ready"), sem("rstd1_ready"), sem("x1_ready")
        x1T_made, x1T_hi_ready, x1T_lo_ready = sem("x1T_made"), sem("x1T_hi_ready"), sem("x1T_lo_ready")
        logits_ready, cent_ready, expo_ready = sem("logits_ready"), sem("cent_ready"), sem("expo_ready")
        gates_ready, gatesT_made, gatesT_ready = sem("gates_ready"), sem("gatesT_made"), sem("gatesT_ready")
        gates_stored, gates_spread = sem("gates_stored"), [sem(f"gates_spread{k}") for k in range(2)]
        h1_ready, h3_ready, silu_ready = sem("h1_ready"), sem("h3_ready"), sem("silu_ready")
        h_ready, h_hi_ready, h_lo_ready, h_used = sem("h_ready"), sem("h_hi_ready"), sem("h_lo_ready"), sem("h_used")
        yT_ready, y_made = sem("yT_ready"), sem("y_made")
        var2_ready, rstd2_ready, o_ready, stored = sem("var2_ready"), sem("rstd2_ready"), sem("o_ready"), sem("stored")
        dve_step = sem("dve_step")

        def qslot(step):
            k = step % 2
            return ps_s[:, k, 0:C], ps_s[:, k, C:2 * C]

        def proj_bank(b, n):
            if b == 0:
                return [ps_s[:, 0, 0:C], ps_s[:, 0, C:2 * C], ps_s[:, 1, 0:C], ps_s[:, 1, C:2 * C],
                        ps_t[:, 0, :], ps_t[:, 1, :]][n]
            return ps_t[:, n % 2, :]

        def x1T_bank(f):
            return ps_z[:, :] if f % 2 == 0 else ps_t[:, 0, :]

        def y_bank(f):
            return ps_z[:, :] if f % 2 else ps_t[:, 1, :]

        block = ctx.enter_context(nc.Block())

        @block.sync
        def _(sp):
            sp.dma_start(xT[:, 0:S], xT_in[:, 0:S]).then_inc(ld_xT[0], 16)
            for n in range(3):
                sp.dma_start(wf[n][:, :], (w1T_in, w3T_in, w2T_in)[n]).then_inc(ld_wf[n], 16)
            sp.dma_start(xs[:, :, :], x.rearrange("b (t p) d -> p (b t) d", p=P)).then_inc(ld_x, 16)
            sp.dma_start(xT[:, S:2 * S], xT_in[:, S:2 * S]).then_inc(ld_xT[1], 16)

            def spread_gates(f):
                sp.wait_ge(gatesT_ready, f + 1)
                sp.dma_start(gates_dram[f], gatesT[0:CT * E, f, :]).then_inc(gates_stored, 16)
                sp.wait_ge(gates_stored, 16 * (f + 1))
                if f >= 2:
                    sp.wait_ge(h_ready, NE * (f - 1))
                sp.dma_start(gspread[:, f % 2], gates_dram[f].rearrange("(t e) q -> t e q", e=E)
                             .partition_broadcast(P)).then_inc(gates_spread[f % 2], 16)

            def store(f):
                sp.wait_ge(o_ready, f + 1)
                sp.dma_start(out.rearrange("b (t p) d -> p (b t) d", p=P)[:, CT * f:CT * (f + 1), :],
                             o[:, CT * f:CT * (f + 1), :]).then_inc(stored, 16)

            for b in range(B):
                spread_gates(2 * b)
                spread_gates(2 * b + 1)
                store(2 * b)
                store(2 * b + 1)
            sp.wait_ge(stored, 16 * NCH)

        @block.gpsimd
        def _(pool):
            steps = [0]

            def link(ins):
                steps[0] += 1
                ins.then_inc(pool_step, 1)
                pool.wait_ge(pool_step, steps[0])

            link(nc.gpsimd.memset(ident[:, :], 0.0))
            nc.gpsimd.affine_select(out=ident[:, :], in_=ident[:, :], compare_op=ALU.not_equal, fill=1.0,
                                    base=0, pattern=[[-1, P]], channel_multiplier=1).then_inc(consts_ready, 1)
            link(nc.gpsimd.memset(ident16[:, :], 0.0))
            nc.gpsimd.affine_select(out=ident16[:, :], in_=ident16[:, :], compare_op=ALU.not_equal, fill=1.0,
                                    base=0, pattern=[[-1, P]], channel_multiplier=1).then_inc(consts_ready, 1)
            link(nc.gpsimd.memset(mask16[:, :], 0.0))
            nc.gpsimd.affine_select(out=mask16[:, :], in_=mask16[:, :], compare_op=ALU.is_ge, fill=MASKED,
                                    base=0, pattern=[[-1, P]], channel_multiplier=1).then_inc(consts_ready, 1)
            nc.gpsimd.iota(expert_no[:, :, :], pattern=[[0, CT], [1, E]], base=0,
                           channel_multiplier=0).then_inc(consts_ready, 1)
            nc.gpsimd.memset(gates[:, :, :], 0.0).then_inc(consts_ready, 1)
            nc.gpsimd.memset(minus_half[:, :], -0.5)
            link(nc.gpsimd.memset(euler[:, :, :], EULER))

            for n in range(3):
                pool.wait_ge(w_hi_ready, n + 1)
                nc.gpsimd.tensor_tensor(wf_lo[n][:, :], wf[n][:, :], wf_hi[n][:, :].bitcast(f32),
                                        ALU.subtract).then_inc(w_lo_ready, 1)

            def rstd(f, var_ready, ve, to, ready):
                pool.wait_ge(var_ready, f + 1)
                nc.gpsimd.tensor_tensor(to[:, CT * f:CT * (f + 1)], ve[:, CT * f:CT * (f + 1)],
                                        minus_half[:, :], ALU.pow).then_inc(ready, 1)

            def router_exp(f):
                pool.wait_ge(cent_ready, f + 1)
                nc.gpsimd.tensor_tensor(expo[:, f], euler[:, :, :], cent[:, f], ALU.pow).then_inc(expo_ready, 1)

            for b in range(B):
                for f in (2 * b, 2 * b + 1):
                    rstd(f, var1_ready, ve1, rstd1, rstd1_ready)
                    router_exp(f)
                for f in (2 * b, 2 * b + 1):
                    rstd(f, var2_ready, ve2, rstd2, rstd2_ready)

        @block.scalar
        def _(act):
            act.dma_start(watt[:, :], w_att).then_inc(ld_watt, 16)
            act.dma_start(bqk[:, :], b_qk).then_inc(ld_bias, 16)
            act.dma_start(bv[:, :], b_v.partition_broadcast(P)).then_inc(ld_bias, 16)
            act.dma_start(gw[:, :], gate_wT).then_inc(ld_bias, 16)
            act.dma_start(gb[:, :], gate_b.partition_broadcast(P)).then_inc(ld_bias, 16)

            def kq_out(b, n):
                c, q = n // 2, n % 2
                act.wait_ge(proj_ready, 6 * b + n + 1)
                nc.scalar.activation((qT if q else kT)[:, C * c:C * (c + 1)], proj_bank(b, n), ACT.Identity,
                                     bias=bqk[:, 1 - q:2 - q]).then_inc(kq_ready, 1)

            def exp(b, i):
                g = b * ST + i
                act.wait_ge(negmax_ready, g + 1)
                if g >= 2:
                    act.wait_ge(pT_made, GPS * ((g - 2) // ST) + G0[(g - 2) % ST + 1])
                w = (i + 1) * P
                nc.scalar.activation(probs[:, g % 2, 0:w], ps_s[:, g % 2, 0:w], ACT.Exp,
                                     bias=negmax[:, g:g + 1], accum_out=rowsum[:, g:g + 1]).then_inc(probs_ready, 1)

            def pT_out(b, i):
                for g, (j0, j1) in enumerate(GROUPS[i]):
                    n = G0[i] + g
                    if not by_act(n):
                        continue
                    act.wait_ge(pT_made, GPS * b + n + 1)
                    q = i % CT
                    nc.scalar.copy(pT[:, j0 + i // CT * CT:j1 + i // CT * CT, P * q:P * (q + 1)],
                                   ps_t[:, n % 2, 0:P * (j1 - j0)].rearrange("p (j q) -> p j q", q=P)
                                   ).then_inc(pT_by_act, 1)

            def zT_out(f):
                act.wait_ge(zT_made, f + 1)
                nc.scalar.copy(zT[:, f % 2], ps_z[:, :]).then_inc(zT_ready, 1)

            def x1T_high(f):
                act.wait_ge(x1T_made, f + 1)
                nc.scalar.copy(x1T_hi[:, f % 2], x1T_bank(f)).then_inc(x1T_hi_ready, 1)

            def gatesT_out(f):
                act.wait_ge(gatesT_made, f + 1)
                nc.scalar.copy(gatesT[:, f], ps_m[:, 0:P]).then_inc(gatesT_ready, 1)

            def yT_out(f):
                act.wait_ge(h_used, NE * (f + 1))
                nc.scalar.copy(yT[:, f % 2], ps_y[f % 2][:, :]).then_inc(yT_ready, 1)

            def silu_step(m):
                act.wait_ge(h1_ready, m + 1)
                if m >= 3:
                    act.wait_ge(h_ready, m - 2)
                nc.scalar.activation(silu[:, m % 3], qslot(m)[0], ACT.Silu).then_inc(silu_ready, 1)

            def h_high(m):
                act.wait_ge(h_ready, m + 1)
                if m >= 3:
                    act.wait_ge(h_used, m - 2)
                nc.scalar.copy(h_hi[:, m % 3], h[:, m % 3]).then_inc(h_hi_ready, 1)

            def w_high(n):
                act.wait_ge(ld_wf[n], 16)
                nc.scalar.copy(wf_hi[n][:, :], wf[n][:, :]).then_inc(w_hi_ready, 1)

            act.wait_ge(ld_bias, 64)
            act.wait_ge(watt_ready, 2)
            for n in range(4):
                kq_out(0, n)
            for b in range(B):
                f = 2 * b
                exp(b, 0)
                for i in range(ST):
                    if i == CT + 1:
                        zT_out(f)
                    if i + 1 < ST:
                        exp(b, i + 1)
                    if b and i == 0:
                        yT_out(f - 1)
                    if not b and i < 3:
                        w_high(i)
                    if i == ST - 1:
                        x1T_high(f)
                    pT_out(b, i)
                zT_out(f + 1)
                gatesT_out(f)
                for step in range(2 * NE):
                    c, e = divmod(step, NE)
                    m = NE * f + step
                    if c and e == 2:
                        yT_out(f)
                    silu_step(m)
                    if step:
                        h_high(m - 1)
                    if c == 0 and e == 3:
                        x1T_high(f + 1)
                    if c == 0 and e == 7:
                        gatesT_out(f + 1)
                    if c and b + 1 < B and 4 <= e < 8:
                        kq_out(b + 1, e - 4)
                h_high(m)
            yT_out(NCH - 1)

        @block.vector
        def _(dve):
            steps = [0]

            def link(ins):
                steps[0] += 1
                ins.then_inc(dve_step, 1)
                dve.wait_ge(dve_step, steps[0])

            def row_max(b, i):
                g = b * ST + i
                dve.wait_ge(scores_ready, g + 1)
                nc.vector.tensor_reduce(negmax[:, g:g + 1], ps_s[:, g % 2, 0:(i + 1) * P], AX.X, ALU.max,
                                        negate=True).then_inc(negmax_ready, 1)

            def pT_out(b, i):
                for g, (j0, j1) in enumerate(GROUPS[i]):
                    n = G0[i] + g
                    if by_act(n):
                        continue
                    dve.wait_ge(pT_made, GPS * b + n + 1)
                    q = i % CT
                    nc.vector.tensor_copy(pT[:, j0 + i // CT * CT:j1 + i // CT * CT, P * q:P * (q + 1)],
                                          ps_t[:, n % 2, 0:P * (j1 - j0)].rearrange("p (j q) -> p j q", q=P)
                                          ).then_inc(pT_by_dve, 1)

            def v_out(b, n):
                dve.wait_ge(proj_ready, 6 * b + 5 + n)
                nc.vector.tensor_tensor(v[:, CT * n:CT * (n + 1), :],
                                        proj_bank(b, 4 + n).rearrange("p (t d) -> p t d", d=D),
                                        bv[:, :].unsqueeze(1).to_broadcast([P, CT, D]), ALU.add).then_inc(v_ready, 1)

            def norm_stats(f, y, mv, ve, ready):
                for t in range(CT):
                    last = nc.vector.bn_stats(stats[:, f % 2, t, :], y[:, CT * f + t, :])
                link(last)
                for t in range(CT):
                    last = nc.vector.bn_aggr(mv[:, CT * f + t, :], stats[:, f % 2, t, :])
                link(last)
                nc.vector.tensor_scalar(ve[:, CT * f:CT * (f + 1)], mv[:, CT * f:CT * (f + 1), 1], EPS, None,
                                        ALU.add).then_inc(ready, 1)

            def norm_apply(f, y, mv, rstd, rstd_ready, to, ready):
                dve.wait_ge(rstd_ready, f + 1)
                for t in range(CT * f, CT * (f + 1)):
                    last = nc.vector.tensor_scalar(to[:, t, :], y[:, t, :], mv[:, t, 0:1], rstd[:, t:t + 1],
                                                   ALU.subtract, ALU.mult)
                last.then_inc(ready, 1)

            def norm1_stats(f):
                dve.wait_ge(probs_ready, CT * (f + 1))
                link(nc.vector.reciprocal(rinv[:, CT * f:CT * (f + 1)], rowsum[:, CT * f:CT * (f + 1)]))
                dve.wait_ge(z_made, f + 1)
                dve.wait_ge(ld_x, 16)
                for t in range(CT):
                    g = CT * f + t
                    last = nc.vector.scalar_tensor_tensor(y1[:, g, :], ps_m[:, P * t:P * (t + 1)], rinv[:, g:g + 1],
                                                          xs[:, g, :], ALU.mult, ALU.add)
                link(last)
                norm_stats(f, y1, mv1, ve1, var1_ready)

            def norm1_apply(f):
                norm_apply(f, y1, mv1, rstd1, rstd1_ready, x1, x1_ready)

            def x1T_low(f):
                dve.wait_ge(x1T_hi_ready, f + 1)
                nc.vector.tensor_tensor(x1T_lo[:, f % 2], x1T_bank(f), x1T_hi[:, f % 2].bitcast(f32),
                                        ALU.subtract).then_inc(x1T_lo_ready, 1)

            def router_centre(f):
                dve.wait_ge(logits_ready, f + 1)
                lg = ps_m[:, 0:CT * E].rearrange("p (t e) -> p t e", e=E)
                link(nc.vector.tensor_reduce(lmax[:, :], lg, AX.X, ALU.max))
                nc.vector.tensor_tensor(cent[:, f], lg, lmax[:, :].unsqueeze(2).to_broadcast([P, CT, E]),
                                        ALU.subtract).then_inc(cent_ready, 1)

            def router_gates(f):
                dve.wait_ge(expo_ready, f + 1)
                link(nc.vector.tensor_reduce(esum[:, :], expo[:, f], AX.X, ALU.add))
                link(nc.vector.reciprocal(einv[:, :], esum[:, :]))
                link(nc.vector.tensor_tensor(score[:, :, :], expo[:, f],
                                             einv[:, :].unsqueeze(2).to_broadcast([P, CT, E]), ALU.mult))
                link(nc.vector.tensor_tensor(biased[:, :, :], score[:, :, :],
                                             gb[:, :].unsqueeze(1).to_broadcast([P, CT, E]), ALU.add))
                for t in range(CT):
                    last = nc.vector.max(top[:, t, :], biased[:, t, :])
                link(last)
                for t in range(CT):
                    last = nc.vector.max_index(topi[:, t, :], top[:, t, :], biased[:, t, :])
                link(last)
                nc.vector.tensor_tensor(is0[:, :, :], expert_no[:, :, :],
                                        topi[:, :, 0:1].to_broadcast([P, CT, E]), ALU.is_equal)
                link(nc.vector.tensor_tensor(is1[:, :, :], expert_no[:, :, :],
                                             topi[:, :, 1:2].to_broadcast([P, CT, E]), ALU.is_equal))
                link(nc.vector.tensor_tensor(is0[:, :, :], is0[:, :, :], is1[:, :, :], ALU.add))
                nc.vector.tensor_tensor(gates[:, f, 0:CT * E].rearrange("p (t e) -> p t e", e=E),
                                        score[:, :, :], is0[:, :, :], ALU.mult).then_inc(gates_ready, 1)

            def h_step(m):
                f, e = divmod(m, NE)
                dve.wait_ge(silu_ready, m + 1)
                s = silu[:, m % 3]
                if e >= SH:
                    if e == SH:
                        dve.wait_ge(gates_spread[f % 2], 16 * (f // 2 + 1))
                    link(nc.vector.tensor_tensor(s.rearrange("p (t q) -> p t q", q=P),
                                                 s.rearrange("p (t q) -> p t q", q=P),
                                                 gspread[:, f % 2, :, e - SH, :], ALU.mult))
                dve.wait_ge(h3_ready, m + 1)
                if m >= 3:
                    dve.wait_ge(h_hi_ready, m - 2)
                nc.vector.tensor_tensor(h[:, m % 3], s, qslot(m)[1], ALU.mult).then_inc(h_ready, 1)

            def h_low(m):
                dve.wait_ge(h_hi_ready, m + 1)
                nc.vector.tensor_tensor(h_lo[:, m % 3], h[:, m % 3], h_hi[:, m % 3].bitcast(f32),
                                        ALU.subtract).then_inc(h_lo_ready, 1)

            def norm2_stats(f):
                dve.wait_ge(y_made, f + 1)
                link(nc.vector.tensor_tensor(y2[:, CT * f:CT * (f + 1), :],
                                             y_bank(f).rearrange("p (t d) -> p t d", d=D),
                                             x1[:, CT * f:CT * (f + 1), :], ALU.add))
                norm_stats(f, y2, mv2, ve2, var2_ready)

            def norm2_apply(f):
                norm_apply(f, y2, mv2, rstd2, rstd2_ready, o, o_ready)

            dve.wait_ge(ld_watt, 16)
            nc.vector.tensor_scalar(watt[:, P:2 * P], watt[:, P:2 * P], SCALE, None, ALU.mult).then_inc(watt_ready, 1)
            dve.wait_ge(ld_bias, 64)
            nc.vector.tensor_scalar(bqk[:, 0:1], bqk[:, 0:1], SCALE, None, ALU.mult).then_inc(watt_ready, 1)
            link(nc.vector.tensor_copy(gw_hi[:, :], gw[:, :]))
            nc.vector.tensor_tensor(gw_lo[:, :], gw[:, :], gw_hi[:, :].bitcast(f32), ALU.subtract)
            v_out(0, 0)
            v_out(0, 1)
            dve.wait_ge(consts_ready, 5)
            for b in range(B):
                f = 2 * b
                row_max(b, 0)
                for i in range(ST):
                    if i + 1 < ST:
                        row_max(b, i + 1)
                    pT_out(b, i)
                    if b and i == 1:
                        norm2_stats(f - 1)
                    if b and i == 2:
                        norm2_apply(f - 1)
                    if i == CT + 1:
                        norm1_stats(f)
                    if i == CT + 2:
                        norm1_apply(f)
                x1T_low(f)
                router_centre(f)
                router_gates(f)
                for c in range(2):
                    for e in range(NE):
                        m = NE * (f + c) + e
                        h_step(m)
                        if c or e:
                            h_low(m - 1)
                        if c == 0:
                            if e == 0:
                                norm1_stats(f + 1)
                            elif e == 1:
                                norm1_apply(f + 1)
                            elif e == 3:
                                x1T_low(f + 1)
                            elif e == 5:
                                router_centre(f + 1)
                            elif e == 6:
                                router_gates(f + 1)
                        else:
                            if e == 4:
                                norm2_stats(f)
                            elif e == 5:
                                norm2_apply(f)
                            elif b + 1 < B and e >= 8:
                                v_out(b + 1, e - 8)
                h_low(m)
            norm2_stats(NCH - 1)
            norm2_apply(NCH - 1)

        @block.tensor
        def _(pe):
            mm = nc.tensor.matmul

            def project(b, n):
                if n == 0:
                    pe.wait_ge(ld_xT[b], 16)
                if b and n == 1:
                    pe.wait_ge(var2_ready, 2 * b - 1)
                if b and n >= 2:
                    pe.wait_ge(kq_ready, 4 * b + n - 1)
                to = proj_bank(b, n)
                if n < 4:
                    c, q = n // 2, n % 2
                    mm(to, watt[:, P * q:P * (q + 1)], xT[:, S * b + C * c:S * b + C * (c + 1)],
                       start=True, stop=True).then_inc(proj_ready, 1)
                else:
                    for t in range(CT):
                        tok = S * b + C * (n - 4) + P * t
                        last = mm(to[:, P * t:P * (t + 1)], xT[:, tok:tok + P], watt[:, 2 * P:3 * P],
                                  start=True, stop=True)
                    last.then_inc(proj_ready, 1)

            def scores(b, i):
                g = b * ST + i
                if i < 2:
                    pe.wait_ge(kq_ready, 4 * b + (2 if i == 0 else 4))
                if g >= 2 and i >= 2:
                    pe.wait_ge(probs_ready, g - 1)
                if b and i < 2:
                    pe.wait_ge(h_ready, NE * 2 * b - 1 + i)
                q = qT[:, P * i:P * (i + 1)]
                for k0 in range(0, (i + 1) * P, C):
                    k1 = min(k0 + C, (i + 1) * P)
                    diagonal = k1 == (i + 1) * P
                    last = mm(ps_s[:, g % 2, k0:k1], q, kT[:, k0:k1], start=True, stop=not diagonal)
                last = mm(ps_s[:, g % 2, P * i:P * (i + 1)], ident16[:, :], mask16[:, :], start=False, stop=True)
                last.then_inc(scores_ready, 1)

            def transpose_probs(b, i):
                g = b * ST + i
                pe.wait_ge(probs_ready, g + 1)
                for k, (j0, j1) in enumerate(GROUPS[i]):
                    n = G0[i] + k
                    if n < 2:
                        pe.wait_ge(v_ready, 2 * b + n + 1)
                    else:
                        a = by_act(n - 2)
                        pe.wait_ge(pT_by_act if a else pT_by_dve, groups_of(a, GPS * b + n - 1))
                    for j in range(j0, j1):
                        last = nc.tensor.transpose(ps_t[:, n % 2, P * (j - j0):P * (j - j0 + 1)],
                                                   probs[:, g % 2, P * j:P * (j + 1)], ident[:, :])
                    last.then_inc(pT_made, 1)

            def attend(b, c):
                f = 2 * b + c
                upto = GPS * b + G0[CT * (c + 1)]
                pe.wait_ge(pT_by_act, groups_of(True, upto))
                pe.wait_ge(pT_by_dve, groups_of(False, upto))
                if c:
                    pe.wait_ge(x1T_lo_ready, f)
                tiles = CT * (c + 1)
                for j in range(tiles):
                    q0 = P * max(0, j - CT * c)
                    last = mm(ps_z[:, q0:C], v[:, j, :], pT[:, CT * c + j, q0:C], start=j == 0, stop=j == tiles - 1)
                last.then_inc(zT_made, 1)

            def transpose4(to, src):
                for t in range(CT):
                    last = nc.tensor.transpose(to[:, P * t:P * (t + 1)], src(t), ident[:, :])
                return last

            def transpose_z(f):
                pe.wait_ge(zT_ready, f + 1)
                if f % 2:
                    pe.wait_ge(gatesT_ready, f)
                transpose4(ps_m, lambda t: zT[:, f % 2, P * t:P * (t + 1)]).then_inc(z_made, 1)

            def transpose_x1(f):
                pe.wait_ge(x1_ready, f + 1)
                transpose4(x1T_bank(f), lambda t: x1[:, CT * f + t, :]).then_inc(x1T_made, 1)

            def logits(f):
                pe.wait_ge(x1T_lo_ready, f + 1)
                for t in range(CT):
                    to, hi, lo = ps_m[:, E * t:E * (t + 1)], x1T_hi[:, f % 2, P * t:P * (t + 1)], x1T_lo[:, f % 2, P * t:P * (t + 1)]
                    mm(to, hi, gw_lo[:, :], start=True, stop=False)
                    mm(to, lo, gw_hi[:, :], start=False, stop=False)
                    last = mm(to, hi, gw_hi[:, :], start=False, stop=True)
                last.then_inc(logits_ready, 1)

            def transpose_gates(f):
                pe.wait_ge(gates_ready, f + 1)
                nc.tensor.transpose(ps_m[:, 0:P], gates[:, f, :], ident[:, :]).then_inc(gatesT_made, 1)

            def split_mm(to, n, e, hi, lo, start=True, stop=True):
                w_hi, w_lo = wf_hi[n][:, P * e:P * (e + 1)], wf_lo[n][:, P * e:P * (e + 1)]
                mm(to, w_lo, hi, start=start, stop=False)
                mm(to, w_hi, lo, start=False, stop=False)
                return mm(to, w_hi, hi, start=False, stop=stop)

            def expert_up(m):
                f, e = divmod(m, NE)
                if e == 0:
                    pe.wait_ge(x1T_lo_ready, f + 1)
                    pe.wait_ge(w_lo_ready, 2)
                if m >= 2:
                    pe.wait_ge(h_ready, m - 1)
                if m % (2 * NE) < 2:
                    pe.wait_ge(probs_ready, ST * (f // 2) + ST - 1 + m % 2)
                split_mm(qslot(m)[0], 0, e, x1T_hi[:, f % 2], x1T_lo[:, f % 2]).then_inc(h1_ready, 1)
                split_mm(qslot(m)[1], 1, e, x1T_hi[:, f % 2], x1T_lo[:, f % 2]).then_inc(h3_ready, 1)

            def expert_down(m):
                f, e = divmod(m, NE)
                pe.wait_ge(h_lo_ready, m + 1)
                if e == 0:
                    pe.wait_ge(w_lo_ready, 3)
                    if f % 2:
                        pe.wait_ge(gatesT_ready, f + 1)
                    else:
                        pe.wait_ge(zT_ready, f + 2)
                last = split_mm(ps_y[f % 2][:, :], 2, e, h_hi[:, m % 3], h_lo[:, m % 3],
                                start=e == 0, stop=e == NE - 1)
                last.then_inc(h_used, 1)

            def transpose_y(f):
                pe.wait_ge(yT_ready, f + 1)
                transpose4(y_bank(f), lambda t: yT[:, f % 2, P * t:P * (t + 1)]).then_inc(y_made, 1)

            pe.wait_ge(watt_ready, 1)
            for n in range(6):
                project(0, n)
            pe.wait_ge(consts_ready, 3)
            scores(0, 0)
            for b in range(B):
                f = 2 * b
                for i in range(ST):
                    if i + 1 < ST and (b == 0 or i):
                        scores(b, i + 1)
                    if i == ST - 1:
                        transpose_x1(f)
                    transpose_probs(b, i)
                    if b and i == 0:
                        transpose_y(f - 1)
                    if i == CT:
                        attend(b, 0)
                    if i == CT + 1:
                        transpose_z(f)
                logits(f)
                attend(b, 1)
                transpose_gates(f)
                for c in range(2):
                    for e in range(NE):
                        m = NE * (f + c) + e
                        expert_up(m)
                        if c or e >= 2:
                            expert_down(m - 2)
                        if c == 0:
                            if e == 0:
                                transpose_z(f + 1)
                            elif e == 3:
                                transpose_x1(f + 1)
                            elif e == 4:
                                logits(f + 1)
                            elif e == 7:
                                transpose_gates(f + 1)
                        else:
                            if e == 3:
                                transpose_y(f)
                            elif b + 1 < B and e >= 4:
                                project(b + 1, e - 4)
                for k in (1, 0):
                    if b + 1 < B:
                        scores(b + 1, 1 - k)
                    expert_down(m - k)
            transpose_y(NCH - 1)


def kernel(L0_attn_x, L0_attn_Wq, L0_attn_bq, L0_attn_Wk, L0_attn_bk, L0_attn_Wv, L0_attn_bv, L0_ffn_gate_w,
           L0_ffn_gate_bias, L0_ffn_w1, L0_ffn_w3, L0_ffn_w2, L0_ffn_sw1, L0_ffn_sw3, L0_ffn_sw2):
    import numpy as np
    import concourse.bacc as bacc
    from concourse import mybir as mb
    from concourse.bass_utils import run_bass_kernel_spmd

    x = np.asarray(L0_attn_x)
    B, S, D = x.shape
    up = lambda shared, routed: np.concatenate(
        [np.asarray(shared), np.asarray(routed).reshape(-1, D)], axis=0).T
    down = np.concatenate(
        [np.asarray(L0_ffn_sw2).reshape(D, -1, D).transpose(2, 1, 0), np.asarray(L0_ffn_w2).transpose(2, 0, 1)],
        axis=1).reshape(D, -1)
    ins = {
        "x": x,
        "xT": x.reshape(B * S, D).T,
        "w_att": np.concatenate([np.asarray(w).T for w in (L0_attn_Wk, L0_attn_Wq, L0_attn_Wv)], axis=1),
        "b_qk": np.stack([np.asarray(L0_attn_bq), np.asarray(L0_attn_bk)], axis=1),
        "b_v": np.asarray(L0_attn_bv),
        "gate_wT": np.asarray(L0_ffn_gate_w).T,
        "gate_b": np.asarray(L0_ffn_gate_bias),
        "w1T": up(L0_ffn_sw1, L0_ffn_w1),
        "w3T": up(L0_ffn_sw3, L0_ffn_w3),
        "w2T": down,
    }
    nc = bacc.Bacc("TRN2", target_bir_lowering=False, num_devices=1)
    arrays, args = {}, []
    for name, a in ins.items():
        a = np.ascontiguousarray(a)
        arrays[f"in_{name}_dram"] = a
        args.append(nc.dram_tensor(f"in_{name}_dram", a.shape, mb.dt.from_np(a.dtype), kind="ExternalInput").ap())
    args.append(nc.dram_tensor("out_0_dram", (B, S, D), mb.dt.from_np(x.dtype), kind="ExternalOutput").ap())
    attention_moe_block(nc, *args)
    r = run_bass_kernel_spmd(nc, [arrays], core_ids=[0])
    return r.results[0]["out_0_dram"]
```

```python
import concourse.bass as bass
from concourse import mybir
from contextlib import ExitStack


def attention_moe_block(nc, x, xT_in, w_att, cols_in, rows_in, w1T_in, w3T_in, w2T_in, out):
    f32, f32r, bf16 = mybir.dt.float32, mybir.dt.float32r, mybir.dt.bfloat16
    u32, i32 = mybir.dt.uint32, mybir.dt.int32
    ALU, ACT, AX = mybir.AluOpType, mybir.ActivationFunctionType, mybir.AxisListType

    B, S, D = x.shape
    P = 128
    C = 512
    CT = C // P
    ST = S // P
    NCH = B * S // C
    E = cols_in.shape[1] - 2
    NE = w1T_in.shape[1] // P
    SH = NE - E
    SCALE = float(D) ** -0.5
    EPS = 1e-5
    MASKED = -1e30
    WARM = 9
    FIRST = 2
    SLOTS = 4
    H_SLOTS = 8
    UPS = 3
    STEPS = 2 * NE
    DIRECT = (STEPS - 2, STEPS - 1)
    HIGHS = [[], [0], [1], [2], [], [3, 4], [], [], [5], [6, 7], [], [8, 9, 10, 11], [], [12], [13], [], [14], [15, 16, 17], [], []]
    DOWNS = [0, 0, 1, 0, 1, 0, 0, 1, 1, 0, 0, 4, 2, 1, 0, 1, 1, 0, 2, 1]
    DEFERRED = [2, 0, 0]
    assert D == P and S == 2 * C

    GROUPS = [[(j0, min(j0 + CT, i + 1)) for j0 in range(0, i + 1, CT)] for i in range(ST)]
    G0 = [sum(len(g) for g in GROUPS[:i]) for i in range(ST + 1)]
    GPS = G0[ST]

    def by_act(g):
        return [0, 1, 1, 1, 0, 1, 0, 1, 0, 1, 1, 0][g % GPS] == 1

    def groups_of(act, upto):
        return sum(by_act(g % GPS) == act for g in range(upto))

    gates_dram = nc.dram_tensor("gates_scratch", (NCH, E * CT, P), f32, kind="Internal").ap()

    with ExitStack() as ctx:
        def sb(name, shape, dt=f32):
            return ctx.enter_context(nc.sbuf_tensor(name, shape, dt))

        def sem(name):
            return ctx.enter_context(nc.semaphore(name))

        ident = sb("ident", [P, P])
        ident16 = sb("ident16", [P, P], bf16)
        mask16 = sb("mask16", [P, P], bf16)
        expert_no = sb("expert_no", [P, CT, E], i32)
        minus_half = sb("minus_half", [P, CT])
        watt = sb("watt", [P, 3 * P])
        cols = sb("cols", [P, 2 + E])
        bqk, gw = cols[:, 0:2], cols[:, 2:2 + E]
        rows = sb("rows", [P, D + E])
        bv, gb = rows[:, 0:D], rows[:, D:D + E]
        gw_hi = sb("gw_hi", [P, P], f32r)
        gw_lo = sb("gw_lo", [P, P], f32r)
        wf = [sb(f"w{n}", [P, NE * P]) for n in "132"]
        wf_hi = [sb(f"w{n}_hi", [P, NE * P], f32r) for n in "132"]
        wf_lo = [sb(f"w{n}_lo", [P, NE * P], f32r) for n in "132"]
        xs = sb("xs", [P, B * ST, D])
        xT = sb("xT", [P, B * S])
        kT = sb("kT", [P, S])
        qT = sb("qT", [P, S])
        v = sb("v", [P, ST, D])
        negmax = sb("negmax", [P, B * ST])
        rowsum = sb("rowsum", [P, B * ST])
        rinv = sb("rinv", [P, B * ST])
        probs = sb("probs", [P, 2, S])
        act_slots = sb("act_slots", [P, SLOTS + H_SLOTS, C])
        pT = act_slots[:, 0:4].rearrange("p (s k) c -> p s (k c)", s=2)
        silu, h = act_slots[:, 0:SLOTS], act_slots[:, SLOTS:SLOTS + H_SLOTS]
        y1 = sb("y1", [P, B * ST, D])
        x1 = sb("x1", [P, B * ST, D])
        x1T_hi = sb("x1T_hi", [P, 2, C], f32r)
        x1T_lo = sb("x1T_lo", [P, 2, C], f32r)
        stats = sb("stats", [P, B * ST, 6])
        mv1 = sb("mv1", [P, B * ST, 2])
        mv2 = sb("mv2", [P, B * ST, 2])
        ve1 = sb("ve1", [P, B * ST])
        ve2 = sb("ve2", [P, B * ST])
        rstd1 = sb("rstd1", [P, B * ST])
        rstd2 = sb("rstd2", [P, B * ST])
        logitsT = sb("logitsT", [E, C])
        lmax = sb("lmax", [P, CT])
        cent = sb("cent", [P, NCH, CT, E])
        expo = sb("expo", [P, NCH, CT, E])
        esum = sb("esum", [P, CT])
        einv = sb("einv", [P, CT])
        score = sb("score", [P, CT, E])
        biased = sb("biased", [P, CT, E])
        top = sb("top", [P, CT, 8])
        topi = sb("topi", [P, CT, 8], u32)
        is0 = sb("is0", [P, CT, E])
        is1 = sb("is1", [P, CT, E])
        gates = sb("gates", [P, NCH, P])
        gatesT = sb("gatesT", [P, NCH, P])
        gspread = sb("gspread", [P, 2, E, C])
        h_hi = sb("h_hi", [P, SLOTS, C], f32r)
        h_lo = sb("h_lo", [P, SLOTS, C], f32r)
        warm = sb("warm", [P, C], bf16)
        first_exp = sb("first_exp", [P, 1])
        yT = sb("yT", [P, 2, C])
        y2 = y1
        o = y2

        ps_s = ctx.enter_context(nc.psum_tensor("ps_s", [P, 2, S], f32))
        ps_t = ctx.enter_context(nc.psum_tensor("ps_t", [P, 2, C], f32))
        ps_z = ctx.enter_context(nc.psum_tensor("ps_z", [P, C], f32))
        ps_m = ctx.enter_context(nc.psum_tensor("ps_m", [P, C], f32))
        ps_y = [ps_z, ps_m]
        ps_half = [ps_s[:, k, C:C + C // 2] for k in range(2)]

        consts_ready, zeros_ready, warm_ready = sem("consts_ready"), sem("zeros_ready"), sem("warm_ready")
        pool_step = sem("pool_step")
        ld_xT = [sem(f"ld_xT{k}") for k in range(3)]
        ld_watt, ld_cols, ld_rows, ld_x = sem("ld_watt"), sem("ld_cols"), sem("ld_rows"), sem("ld_x")
        ld_wf = [sem(f"ld_w{n}") for n in "132"]
        watt_ready, w_hi_ready, w_lo_ready = sem("watt_ready"), sem("w_hi_ready"), sem("w_lo_ready")
        kq_made, kq_ready, v_made, v_ready = sem("kq_made"), sem("kq_ready"), sem("v_made"), sem("v_ready")
        scores_ready, negmax_ready, probs_ready = sem("scores_ready"), sem("negmax_ready"), sem("probs_ready")
        pT_made, pT_by_act, pT_by_dve = sem("pT_made"), sem("pT_by_act"), sem("pT_by_dve")
        z_made, rinv_ready, y1_ready = sem("z_made"), sem("rinv_ready"), sem("y1_ready")
        stats1_ready, mv1_ready = sem("stats1_ready"), sem("mv1_ready")
        var1_ready, rstd1_ready, x1_ready = sem("var1_ready"), sem("rstd1_ready"), sem("x1_ready")
        x1T_made, x1T_hi_ready, x1T_lo_ready = sem("x1T_made"), sem("x1T_hi_ready"), sem("x1T_lo_ready")
        logitsT_made, logitsT_ready, logits_ready = sem("logitsT_made"), sem("logitsT_ready"), sem("logits_ready")
        cent_ready, expo_ready = sem("cent_ready"), sem("expo_ready")
        gates_ready, gatesT_made, gatesT_ready = sem("gates_ready"), sem("gatesT_made"), sem("gatesT_ready")
        gates_stored = sem("gates_stored")
        gates_spread = [[sem(f"gates_spread{k}{n}") for n in range(2)] for k in range(2)]
        h1_ready, h3_ready, silu_ready, gated_ready = sem("h1_ready"), sem("h3_ready"), sem("silu_ready"), sem("gated_ready")
        h_ready, h_hi_ready, h_lo_ready, h_used = sem("h_ready"), sem("h_hi_ready"), sem("h_lo_ready"), sem("h_used")
        yT_ready, y_made, y_half_made = sem("yT_ready"), sem("y_made"), sem("y_half_made")
        y2_ready = sem("y2_ready")
        var2_ready, rstd2_ready, o_ready, stored = sem("var2_ready"), sem("rstd2_ready"), sem("o_ready"), sem("stored")
        dve_step = sem("dve_step")

        def split(upto):
            return sum(m % STEPS not in DIRECT for m in range(upto))

        def expert(m):
            f, k = divmod(m, NE)
            return (k + SH) % NE if f % 2 else k

        def gated(upto):
            return sum(expert(m) >= SH for m in range(upto))

        def up_banks(m):
            k = m % STEPS % UPS
            return (ps_t[:, 0, :], ps_t[:, 1, :]) if k == 2 else (ps_s[:, k, 0:C], ps_s[:, k, C:2 * C])

        def proj_bank(b, n):
            if b == 0:
                return [ps_s[:, 0, 0:C], ps_s[:, 0, C:2 * C], ps_z[:, :], ps_m[:, :], ps_t[:, 0, :], ps_m[:, :]][n]
            return ps_s[:, 0, C * n:C * (n + 1)] if n < 2 else ps_t[:, n % 2, :]

        block = ctx.enter_context(nc.Block())

        @block.sync
        def _(sp):
            sp.dma_start(xT[:, 0:C], xT_in[:, 0:C]).then_inc(ld_xT[0], 16)
            sp.dma_start(xT[:, C:S], xT_in[:, C:S]).then_inc(ld_xT[1], 16)
            for n in range(3):
                sp.dma_start(wf[n][:, :], (w1T_in, w3T_in, w2T_in)[n]).then_inc(ld_wf[n], 16)
            sp.dma_start(xs[:, :, :], x.rearrange("b (t p) d -> p (b t) d", p=P)).then_inc(ld_x, 16)
            sp.dma_start(xT[:, S:2 * S], xT_in[:, S:2 * S]).then_inc(ld_xT[2], 16)

            def spread_gates(f):
                sp.wait_ge(gatesT_ready, f + 1)
                sp.dma_start(gates_dram[f], gatesT[0:CT * E, f, :]).then_inc(gates_stored, 16)
                sp.wait_ge(gates_stored, 16 * (f + 1))
                if f >= 2:
                    sp.wait_ge(gated_ready, E * (f - 1))
                g = gates_dram[f].rearrange("(e t) q -> e (t q)", t=CT)
                for n, (e0, e1) in enumerate(((0, FIRST), (FIRST, E))):
                    sp.dma_start(gspread[:, f % 2, e0:e1, :], g[e0:e1].partition_broadcast(P)
                                 ).then_inc(gates_spread[f % 2][n], 16)

            def store(f, part=0, parts=1):
                sp.wait_ge(o_ready, f + part + 1)
                t0, t1 = CT * f + CT // parts * part, CT * f + CT // parts * (part + 1)
                sp.dma_start(out.rearrange("b (t p) d -> p (b t) d", p=P)[:, t0:t1, :], o[:, t0:t1, :]
                             ).then_inc(stored, 16)

            for b in range(B):
                spread_gates(2 * b)
                spread_gates(2 * b + 1)
                store(2 * b)
                if b + 1 < B:
                    store(2 * b + 1)
            store(NCH - 1, 0, 2)
            store(NCH - 1, 1, 2)
            sp.wait_ge(stored, 16 * (NCH + 1))

        @block.gpsimd
        def _(pool):
            steps = [0]

            def link(ins):
                steps[0] += 1
                ins.then_inc(pool_step, 1)
                pool.wait_ge(pool_step, steps[0])

            link(nc.gpsimd.memset(ident[:, :], 0.0))
            nc.gpsimd.affine_select(out=ident[:, :], in_=ident[:, :], compare_op=ALU.not_equal, fill=1.0,
                                    base=0, pattern=[[-1, P]], channel_multiplier=1).then_inc(consts_ready, 1)
            link(nc.gpsimd.memset(ident16[:, :], 0.0))
            nc.gpsimd.affine_select(out=ident16[:, :], in_=ident16[:, :], compare_op=ALU.not_equal, fill=1.0,
                                    base=0, pattern=[[-1, P]], channel_multiplier=1).then_inc(consts_ready, 1)
            link(nc.gpsimd.memset(mask16[:, :], 0.0))
            nc.gpsimd.affine_select(out=mask16[:, :], in_=mask16[:, :], compare_op=ALU.is_ge, fill=MASKED,
                                    base=0, pattern=[[-1, P]], channel_multiplier=1).then_inc(consts_ready, 1)
            nc.gpsimd.iota(expert_no[:, :, :], pattern=[[0, CT], [1, E]], base=0,
                           channel_multiplier=0).then_inc(consts_ready, 1)
            nc.gpsimd.memset(gates[:, :, :], 0.0).then_inc(zeros_ready, 1)
            nc.gpsimd.memset(gw_hi[:, :].bitcast(f32), 0.0).then_inc(zeros_ready, 1)
            nc.gpsimd.memset(gw_lo[:, :].bitcast(f32), 0.0).then_inc(zeros_ready, 1)
            link(nc.gpsimd.memset(minus_half[:, :], -0.5))

            def w_low(n):
                pool.wait_ge(w_hi_ready, n + 1)
                nc.gpsimd.tensor_tensor(wf_lo[n][:, :], wf[n][:, :], wf_hi[n][:, :].bitcast(f32),
                                        ALU.subtract).then_inc(w_lo_ready, 1)

            def rstd1_tile(g):
                pool.wait_ge(var1_ready, g + 1)
                nc.gpsimd.tensor_tensor(rstd1[:, g:g + 1], ve1[:, g:g + 1], minus_half[:, 0:1],
                                        ALU.pow).then_inc(rstd1_ready, 1)

            def rstd2_chunk(f):
                pool.wait_ge(var2_ready, f + 1)
                nc.gpsimd.tensor_tensor(rstd2[:, CT * f:CT * (f + 1)], ve2[:, CT * f:CT * (f + 1)],
                                        minus_half[:, :], ALU.pow).then_inc(rstd2_ready, 1)

            def gate(m):
                f, e = m // NE, expert(m)
                if e < SH:
                    return
                if e == SH:
                    pool.wait_ge(gates_spread[f % 2][0], 16 * (f // 2 + 1))
                if e == SH + FIRST:
                    pool.wait_ge(gates_spread[f % 2][1], 16 * (f // 2 + 1))
                pool.wait_ge(h_ready, m + 1)
                nc.gpsimd.tensor_tensor(h[:, m % H_SLOTS], h[:, m % H_SLOTS], gspread[:, f % 2, e - SH, :],
                                        ALU.mult).then_inc(gated_ready, 1)

            for b in range(B):
                f = 2 * b
                for i in range(ST):
                    if b == 0 and i < 3:
                        w_low(i)
                    if b and i == 2 + 1:
                        rstd2_chunk(f - 1)
                    rstd1_tile(ST * b + i)
                for step in range(STEPS):
                    gate(NE * f + step)
                    if step == 17:
                        rstd2_chunk(f)
            for k in range(2):
                pool.wait_ge(var2_ready, NCH + k)
                t0 = B * ST - CT + CT // 2 * k
                nc.gpsimd.tensor_tensor(rstd2[:, t0:t0 + CT // 2], ve2[:, t0:t0 + CT // 2],
                                        minus_half[:, 0:CT // 2], ALU.pow).then_inc(rstd2_ready, 1)

        @block.scalar
        def _(act):
            act.dma_start(watt[:, :], w_att).then_inc(ld_watt, 16)
            act.dma_start(cols[:, :], cols_in).then_inc(ld_cols, 16)
            act.dma_start(rows[:, :], rows_in.partition_broadcast(P)).then_inc(ld_rows, 16)

            def kq_out(b, n):
                c, q = n // 2, n % 2
                act.wait_ge(kq_made, 4 * b + n + 1)
                nc.scalar.activation((qT if q else kT)[:, C * c:C * (c + 1)], proj_bank(b, n), ACT.Identity,
                                     bias=bqk[:, 1 - q:2 - q]).then_inc(kq_ready, 1)

            def exp(b, i):
                g = b * ST + i
                act.wait_ge(negmax_ready, g + 1)
                if g >= 2:
                    act.wait_ge(pT_made, GPS * ((g - 2) // ST) + G0[(g - 2) % ST + 1])
                w = (i + 1) * P
                nc.scalar.activation(probs[:, g % 2, 0:w], ps_s[:, g % 2, 0:w], ACT.Exp,
                                     bias=negmax[:, g:g + 1], accum_out=rowsum[:, g:g + 1]).then_inc(probs_ready, 1)

            def pT_out(b, i):
                for g, (j0, j1) in enumerate(GROUPS[i]):
                    n = G0[i] + g
                    if not by_act(n):
                        continue
                    act.wait_ge(pT_made, GPS * b + n + 1)
                    nc.scalar.copy(pT[:, i % 2, P * j0:P * j1], ps_t[:, n % 2, 0:P * (j1 - j0)]).then_inc(pT_by_act, 1)

            def x1T_high(f):
                act.wait_ge(x1T_made, f + 1)
                nc.scalar.copy(x1T_hi[:, f % 2], ps_m[:, :]).then_inc(x1T_hi_ready, 1)

            def logitsT_out(f):
                act.wait_ge(logitsT_made, f + 1)
                nc.scalar.copy(logitsT[:, :], ps_m[0:E, :]).then_inc(logitsT_ready, 1)

            def router_exp(f):
                act.wait_ge(cent_ready, f + 1)
                nc.scalar.activation(expo[:, f], cent[:, f], ACT.Exp).then_inc(expo_ready, 1)

            def gatesT_out(f):
                act.wait_ge(gatesT_made, f + 1)
                nc.scalar.copy(gatesT[:, f], ps_m[:, 0:P]).then_inc(gatesT_ready, 1)

            def yT_out(f):
                act.wait_ge(h_used, split(NE * (f + 1)))
                nc.scalar.copy(yT[:, f % 2], ps_y[f % 2][:, :]).then_inc(yT_ready, 1)

            def silu_step(m):
                act.wait_ge(h1_ready, m + 1)
                if m >= SLOTS:
                    act.wait_ge(h_ready, m - SLOTS + 1)
                nc.scalar.activation(silu[:, m % SLOTS], up_banks(m)[0], ACT.Silu).then_inc(silu_ready, 1)

            def h_high(m):
                if m % STEPS in DIRECT:
                    return
                if expert(m) < SH:
                    act.wait_ge(h_ready, m + 1)
                else:
                    act.wait_ge(gated_ready, gated(m + 1))
                if m >= SLOTS:
                    act.wait_ge(h_used, split(m - SLOTS + 1))
                nc.scalar.copy(h_hi[:, m % SLOTS], h[:, m % H_SLOTS]).then_inc(h_hi_ready, 1)

            act.wait_ge(warm_ready, 1)
            nc.scalar.activation(first_exp[:, :], warm[:, 0:1], ACT.Exp)
            act.wait_ge(ld_cols, 16)
            act.wait_ge(watt_ready, 2)
            kq_out(0, 0)
            kq_out(0, 1)
            for b in range(B):
                f = 2 * b
                exp(b, 0)
                for i in range(ST):
                    if i + 1 < ST:
                        exp(b, i + 1)
                    if b == 0 and i < 2:
                        kq_out(0, 2 + i)
                    if b and i == 0:
                        yT_out(f - 1)
                    if 1 and i == 7:
                        logitsT_out(f)
                    pT_out(b, i)
                    if i == 6:
                        x1T_high(f)
                    if b + 1 < B and i == 6:
                        kq_out(b + 1, 0)
                        kq_out(b + 1, 1)
                    if not 1 and i == 7:
                        logitsT_out(f)
                    if i == 7:
                        router_exp(f)
                if b + 1 < B and 1 < 0:
                    kq_out(b + 1, 2)
                    kq_out(b + 1, 3)
                if 8 == 7:
                    router_exp(f)
                if -1 == 1:
                    gatesT_out(f)
                for step in range(STEPS):
                    if step == 1:
                        gatesT_out(f)
                    if step == 2:
                        x1T_high(f + 1)
                    if step == 4:
                        logitsT_out(f + 1)
                    if step == 5:
                        router_exp(f + 1)
                    if b + 1 < B and step == 1:
                        kq_out(b + 1, 2)
                        kq_out(b + 1, 3)
                    silu_step(NE * f + step)
                    if step == 13:
                        yT_out(f)
                    if step == 7:
                        gatesT_out(f + 1)
                    for k in HIGHS[step]:
                        h_high(NE * f + k)
            yT_out(NCH - 1)

        @block.vector
        def _(dve):
            steps = [0]

            def link(ins):
                steps[0] += 1
                ins.then_inc(dve_step, 1)
                dve.wait_ge(dve_step, steps[0])

            def row_max(b, i):
                g = b * ST + i
                dve.wait_ge(scores_ready, g + 1)
                nc.vector.tensor_reduce(negmax[:, g:g + 1], ps_s[:, g % 2, 0:(i + 1) * P], AX.X, ALU.max,
                                        negate=True).then_inc(negmax_ready, 1)

            def pT_out(b, i):
                for g, (j0, j1) in enumerate(GROUPS[i]):
                    n = G0[i] + g
                    if by_act(n):
                        continue
                    dve.wait_ge(pT_made, GPS * b + n + 1)
                    nc.vector.tensor_copy(pT[:, i % 2, P * j0:P * j1], ps_t[:, n % 2, 0:P * (j1 - j0)]
                                          ).then_inc(pT_by_dve, 1)

            def v_out(b, n):
                dve.wait_ge(v_made, 2 * b + n + 1)
                nc.vector.tensor_tensor(v[:, CT * n:CT * (n + 1), :],
                                        proj_bank(b, 4 + n).rearrange("p (t d) -> p t d", d=D),
                                        bv.unsqueeze(1).to_broadcast([P, CT, D]), ALU.add).then_inc(v_ready, 1)

            def norm1_sum(g):
                dve.wait_ge(z_made, g + 1)
                if g == 0:
                    dve.wait_ge(ld_x, 16)
                dve.wait_ge(rinv_ready, g + 1)
                t = g % CT
                nc.vector.scalar_tensor_tensor(y1[:, g, :], ps_z[:, P * t:P * (t + 1)], rinv[:, g:g + 1],
                                               xs[:, g, :], ALU.mult, ALU.add).then_inc(y1_ready, 1)

            def norm1_rinv(g):
                dve.wait_ge(probs_ready, g + 1)
                nc.vector.reciprocal(rinv[:, g:g + 1], rowsum[:, g:g + 1]).then_inc(rinv_ready, 1)

            def norm1_stats(g):
                dve.wait_ge(y1_ready, g + 1)
                nc.vector.bn_stats(stats[:, g, :], y1[:, g, :]).then_inc(stats1_ready, 1)

            def norm1_mean(g):
                dve.wait_ge(stats1_ready, g + 1)
                nc.vector.bn_aggr(mv1[:, g, :], stats[:, g, :]).then_inc(mv1_ready, 1)

            def norm1_var(g):
                dve.wait_ge(mv1_ready, g + 1)
                nc.vector.tensor_scalar(ve1[:, g:g + 1], mv1[:, g, 1:2], EPS, None, ALU.add).then_inc(var1_ready, 1)

            def norm1_apply(g):
                dve.wait_ge(rstd1_ready, g + 1)
                nc.vector.tensor_scalar(x1[:, g, :], y1[:, g, :], mv1[:, g, 0:1], rstd1[:, g:g + 1],
                                        ALU.subtract, ALU.mult).then_inc(x1_ready, 1)

            def x1T_low(f):
                dve.wait_ge(x1T_hi_ready, f + 1)
                nc.vector.tensor_tensor(x1T_lo[:, f % 2], ps_m[:, :], x1T_hi[:, f % 2].bitcast(f32),
                                        ALU.subtract).then_inc(x1T_lo_ready, 1)

            def router_centre(f):
                dve.wait_ge(logits_ready, f + 1)
                lg = ps_m[:, 0:CT * E].rearrange("p (t e) -> p t e", e=E)
                link(nc.vector.tensor_reduce(lmax[:, :], lg, AX.X, ALU.max))
                nc.vector.tensor_tensor(cent[:, f], lg, lmax[:, :].unsqueeze(2).to_broadcast([P, CT, E]),
                                        ALU.subtract).then_inc(cent_ready, 1)

            def router_gates(f):
                dve.wait_ge(consts_ready, 4)
                dve.wait_ge(expo_ready, f + 1)
                link(nc.vector.tensor_reduce(esum[:, :], expo[:, f], AX.X, ALU.add))
                link(nc.vector.reciprocal(einv[:, :], esum[:, :]))
                link(nc.vector.tensor_tensor(score[:, :, :], expo[:, f],
                                             einv[:, :].unsqueeze(2).to_broadcast([P, CT, E]), ALU.mult))
                link(nc.vector.tensor_tensor(biased[:, :, :], score[:, :, :],
                                             gb.unsqueeze(1).to_broadcast([P, CT, E]), ALU.add))
                for t in range(CT):
                    last = nc.vector.max(top[:, t, :], biased[:, t, :])
                link(last)
                for t in range(CT):
                    last = nc.vector.max_index(topi[:, t, :], top[:, t, :], biased[:, t, :])
                link(last)
                nc.vector.tensor_tensor(is0[:, :, :], expert_no[:, :, :],
                                        topi[:, :, 0:1].to_broadcast([P, CT, E]), ALU.is_equal)
                link(nc.vector.tensor_tensor(is1[:, :, :], expert_no[:, :, :],
                                             topi[:, :, 1:2].to_broadcast([P, CT, E]), ALU.is_equal))
                link(nc.vector.tensor_tensor(is0[:, :, :], is0[:, :, :], is1[:, :, :], ALU.add))
                nc.vector.tensor_tensor(gates[:, f, 0:CT * E].rearrange("p (e t) -> p t e", t=CT),
                                        score[:, :, :], is0[:, :, :], ALU.mult).then_inc(gates_ready, 1)

            def h_step(m):
                dve.wait_ge(silu_ready, m + 1)
                dve.wait_ge(h3_ready, m + 1)
                if m >= H_SLOTS:
                    dve.wait_ge(h_hi_ready, split(m - H_SLOTS + 1))
                    if (m - H_SLOTS) % STEPS in DIRECT:
                        dve.wait_ge(y_half_made, 2 * (m // STEPS))
                nc.vector.tensor_tensor(h[:, m % H_SLOTS], silu[:, m % SLOTS], up_banks(m)[1],
                                        ALU.mult).then_inc(h_ready, 1)

            def h_low(m):
                if m % STEPS in DIRECT:
                    return
                dve.wait_ge(h_hi_ready, split(m + 1))
                nc.vector.tensor_tensor(h_lo[:, m % SLOTS], h[:, m % H_SLOTS], h_hi[:, m % SLOTS].bitcast(f32),
                                        ALU.subtract).then_inc(h_lo_ready, 1)

            def norm2_sum(f):
                if f % 2:
                    for k in range(2):
                        dve.wait_ge(y_half_made, f + k)
                        t0 = CT * f + CT // 2 * k
                        nc.vector.tensor_tensor(y2[:, t0:t0 + CT // 2, :],
                                                ps_half[k].rearrange("p (t d) -> p t d", d=D),
                                                x1[:, t0:t0 + CT // 2, :], ALU.add).then_inc(y2_ready, 1)
                else:
                    dve.wait_ge(y_made, f // 2 + 1)
                    nc.vector.tensor_tensor(y2[:, CT * f:CT * (f + 1), :],
                                            ps_z[:, :].rearrange("p (t d) -> p t d", d=D),
                                            x1[:, CT * f:CT * (f + 1), :], ALU.add).then_inc(y2_ready, 2)

            def norm2_stats(f):
                dve.wait_ge(y2_ready, 2 * (f + 1))
                for g in range(CT * f, CT * (f + 1)):
                    last = nc.vector.bn_stats(stats[:, g, :], y2[:, g, :])
                link(last)
                for g in range(CT * f, CT * (f + 1)):
                    last = nc.vector.bn_aggr(mv2[:, g, :], stats[:, g, :])
                link(last)
                nc.vector.tensor_scalar(ve2[:, CT * f:CT * (f + 1)], mv2[:, CT * f:CT * (f + 1), 1], EPS, None,
                                        ALU.add).then_inc(var2_ready, 1)

            def norm2_apply(f):
                dve.wait_ge(rstd2_ready, f + 1)
                for g in range(CT * f, CT * (f + 1)):
                    last = nc.vector.tensor_scalar(o[:, g, :], y2[:, g, :], mv2[:, g, 0:1], rstd2[:, g:g + 1],
                                                   ALU.subtract, ALU.mult)
                last.then_inc(o_ready, 1)

            def last_tiles(k):
                return [(ps_half[k][:, P * t:P * (t + 1)], B * ST - CT + CT // 2 * k + t) for t in range(CT // 2)]

            def last_stats(k):
                dve.wait_ge(y_half_made, NCH - 1 + k)
                for y, g in last_tiles(k):
                    last = nc.vector.bn_stats(stats[:, g, :], y)
                link(last)
                for y, g in last_tiles(k):
                    last = nc.vector.bn_aggr(mv2[:, g, :], stats[:, g, :])
                link(last)
                nc.vector.tensor_scalar(ve2[:, g - 1:g + 1], mv2[:, g - 1:g + 1, 1], EPS, None,
                                        ALU.add).then_inc(var2_ready, 1)

            def last_apply(k):
                dve.wait_ge(rstd2_ready, NCH + k)
                for y, g in last_tiles(k):
                    last = nc.vector.tensor_scalar(o[:, g, :], y, mv2[:, g, 0:1], rstd2[:, g:g + 1],
                                                   ALU.subtract, ALU.mult)
                last.then_inc(o_ready, 1)

            def w_high(n):
                dve.wait_ge(ld_wf[n], 16)
                nc.vector.tensor_copy(wf_hi[n][:, :], wf[n][:, :]).then_inc(w_hi_ready, 1)

            nc.vector.memset(warm[:, :], 0.0).then_inc(warm_ready, 1)
            dve.wait_ge(ld_watt, 16)
            nc.vector.tensor_scalar(watt[:, P:2 * P], watt[:, P:2 * P], SCALE, None, ALU.mult).then_inc(watt_ready, 1)
            dve.wait_ge(ld_cols, 16)
            nc.vector.tensor_scalar(bqk[:, 0:1], bqk[:, 0:1], SCALE, None, ALU.mult).then_inc(watt_ready, 1)
            dve.wait_ge(zeros_ready, 3)
            link(nc.vector.tensor_copy(gw_hi[:, 0:E], gw))
            nc.vector.tensor_tensor(gw_lo[:, 0:E], gw, gw_hi[:, 0:E].bitcast(f32), ALU.subtract)
            for b in range(B):
                f = 2 * b
                row_max(b, 0)
                if b == 0:
                    dve.wait_ge(ld_rows, 16)
                    v_out(0, 0)
                for i in range(ST):
                    g = ST * b + i
                    if i + 1 < ST:
                        row_max(b, i + 1)
                    if b and i == 2:
                        norm2_sum(f - 1)
                    norm1_rinv(g)
                    if b == 0 and i == 2:
                        v_out(0, 1)
                    if not 0 and i >= 2:
                        norm1_mean(g - 2)
                    if i >= 1:
                        norm1_sum(g - 1)
                    if not 0 and i >= 2:
                        norm1_var(g - 2)
                    if 0 and i >= 2:
                        norm1_apply(g - 2)
                    if not 0 and i >= 3:
                        norm1_apply(g - 3)
                    if not 1 and i == 6:
                        x1T_low(f)
                    pT_out(b, i)
                    if i >= 1:
                        norm1_stats(g - 1)
                    if b == 0 and i < 3:
                        w_high(i)
                    if i == 7:
                        router_centre(f)
                    if 0 and i >= 1:
                        norm1_mean(g - 1)
                        norm1_var(g - 1)
                    if 1 and i == 6:
                        x1T_low(f)
                    if i == 7:
                        router_gates(f)
                    if b and i == 2 + 1:
                        norm2_stats(f - 1)
                    if b and i == 2 + 3:
                        norm2_apply(f - 1)
                if not 0:
                    norm1_mean(g - 1)
                if 8 == 7:
                    router_centre(f)
                norm1_sum(g)
                if not 0:
                    norm1_var(g - 1)
                norm1_stats(g)
                if not 0:
                    norm1_apply(g - 2)
                norm1_mean(g)
                norm1_apply(g - 1)
                norm1_var(g)
                if 8 == 7:
                    router_gates(f)
                norm1_apply(g)
                if 9 == 7:
                    router_gates(f)
                for step in range(STEPS):
                    m = NE * f + step
                    if step == 2:
                        x1T_low(f + 1)
                    if step == 4:
                        router_centre(f + 1)
                    if step == 5:
                        router_gates(f + 1)
                    h_step(m)
                    for k in HIGHS[step]:
                        h_low(NE * f + k)
                    if step == 13:
                        norm2_sum(f)
                    elif step == 13 + 1:
                        norm2_stats(f)
                    elif step == 19:
                        norm2_apply(f)
                if b + 1 < B:
                    v_out(b + 1, 0)
                    v_out(b + 1, 1)
            for k in range(2):
                last_stats(k)
            for k in range(2):
                last_apply(k)

        @block.tensor
        def _(pe):
            mm = nc.tensor.matmul

            def project(b, n):
                if b:
                    pe.wait_ge(ld_xT[2], 16)
                    if n < 2:
                        pe.wait_ge(probs_ready, ST * b - 1)
                    elif n < 4:
                        pe.wait_ge(pT_by_act, groups_of(True, GPS * b))
                        pe.wait_ge(pT_by_dve, groups_of(False, GPS * b))
                    else:
                        pe.wait_ge(h_ready, STEPS * b - 2)
                else:
                    pe.wait_ge(ld_xT[1 if n in (2, 3, 5) else 0], 16)
                    if n == 5:
                        pe.wait_ge(kq_ready, 4)
                to = proj_bank(b, n)
                if n < 4:
                    c, q = n // 2, n % 2
                    mm(to, watt[:, P * q:P * (q + 1)], xT[:, S * b + C * c:S * b + C * (c + 1)],
                       start=True, stop=True).then_inc(kq_made, 1)
                else:
                    for t in range(CT):
                        tok = S * b + C * (n - 4) + P * t
                        last = mm(to[:, P * t:P * (t + 1)], xT[:, tok:tok + P], watt[:, 2 * P:3 * P],
                                  start=True, stop=True)
                    last.then_inc(v_made, 1)

            def scores(b, i):
                g = b * ST + i
                if i in (0, CT):
                    pe.wait_ge(kq_ready, 4 * b + (4 if i else 2))
                if g >= 2 and i >= 2:
                    pe.wait_ge(probs_ready, g - 1)
                if b and i < 2:
                    pe.wait_ge(h_ready, STEPS * b - 1 + i)
                if b and i in (CT, CT + 1):
                    pe.wait_ge(y2_ready, 4 * b - 1 + i - CT)
                q = qT[:, P * i:P * (i + 1)]
                for k0 in range(0, (i + 1) * P, C):
                    k1 = min(k0 + C, (i + 1) * P)
                    diagonal = k1 == (i + 1) * P
                    last = mm(ps_s[:, g % 2, k0:k1], q, kT[:, k0:k1], start=True, stop=not diagonal)
                last = mm(ps_s[:, g % 2, P * i:P * (i + 1)], ident16[:, :], mask16[:, :], start=False, stop=True)
                last.then_inc(scores_ready, 1)

            def transpose_probs(b, i):
                g = b * ST + i
                pe.wait_ge(probs_ready, g + 1)
                for k, (j0, j1) in enumerate(GROUPS[i]):
                    n = G0[i] + k
                    if n < 2:
                        if b or n == 0:
                            pe.wait_ge(v_ready, 2 * b + n + 1)
                    else:
                        a = by_act(n - 2)
                        pe.wait_ge(pT_by_act if a else pT_by_dve, groups_of(a, GPS * b + n - 1))
                    for j in range(j0, j1):
                        last = nc.tensor.transpose(ps_t[:, n % 2, P * (j - j0):P * (j - j0 + 1)],
                                                   probs[:, g % 2, P * j:P * (j + 1)], ident[:, :])
                    last.then_inc(pT_made, 1)

            def attend(b, i):
                g = ST * b + i
                pe.wait_ge(pT_by_act, groups_of(True, GPS * b + G0[i + 1]))
                pe.wait_ge(pT_by_dve, groups_of(False, GPS * b + G0[i + 1]))
                if i in (0, CT):
                    pe.wait_ge(v_ready, 2 * b + 1 + i // CT)
                if g:
                    pe.wait_ge(y1_ready, g)
                else:
                    pe.wait_ge(kq_ready, 3)
                if b and i == 0:
                    pe.wait_ge(y2_ready, 4 * b - 2)
                t = i % CT
                for j in range(i + 1):
                    last = mm(ps_z[:, P * t:P * (t + 1)], pT[:, i % 2, P * j:P * (j + 1)], v[:, j, :],
                              start=j == 0, stop=j == i)
                last.then_inc(z_made, 1)

            def transpose4(to, src):
                for t in range(CT):
                    last = nc.tensor.transpose(to[:, P * t:P * (t + 1)], src(t), ident[:, :])
                return last

            def transpose_x1(f):
                pe.wait_ge(x1_ready, CT * (f + 1))
                if f % 2:
                    pe.wait_ge(gatesT_ready, f)
                transpose4(ps_m[:, :], lambda t: x1[:, CT * f + t, :]).then_inc(x1T_made, 1)

            def logits_T(f):
                pe.wait_ge(x1T_lo_ready, f + 1)
                hi, lo = x1T_hi[:, f % 2], x1T_lo[:, f % 2]
                mm(ps_m[:, :], gw_lo[:, :], hi, start=True, stop=False)
                mm(ps_m[:, :], gw_hi[:, :], lo, start=False, stop=False)
                mm(ps_m[:, :], gw_hi[:, :], hi, start=False, stop=True).then_inc(logitsT_made, 1)

            def transpose_logits(f):
                pe.wait_ge(logitsT_ready, f + 1)
                for t in range(CT):
                    last = nc.tensor.transpose(ps_m[:, E * t:E * (t + 1)], logitsT[:, P * t:P * (t + 1)],
                                               ident[0:E, 0:E])
                last.then_inc(logits_ready, 1)

            def transpose_gates(f):
                pe.wait_ge(gates_ready, f + 1)
                nc.tensor.transpose(ps_m[:, 0:P], gates[:, f, :], ident[:, :]).then_inc(gatesT_made, 1)

            def split_mm(to, n, e, hi, lo, start=True, stop=True):
                w_hi, w_lo = wf_hi[n][:, P * e:P * (e + 1)], wf_lo[n][:, P * e:P * (e + 1)]
                mm(to, w_lo, hi, start=start, stop=False)
                mm(to, w_hi, lo, start=False, stop=False)
                return mm(to, w_hi, hi, start=False, stop=stop)

            def expert_up(m):
                f, e = m // NE, expert(m)
                step = m % STEPS
                if m % NE == 0:
                    pe.wait_ge(x1T_lo_ready, f + 1)
                    pe.wait_ge(w_lo_ready, 2)
                if step >= UPS:
                    pe.wait_ge(h_ready, m - UPS + 1)
                elif step < 2:
                    pe.wait_ge(probs_ready, ST * (f // 2 + 1) - 1 + step)
                else:
                    pe.wait_ge(pT_by_act, groups_of(True, GPS * (f // 2 + 1)))
                    pe.wait_ge(pT_by_dve, groups_of(False, GPS * (f // 2 + 1)))
                if step in (0, 2):
                    pe.wait_ge(kq_ready, min(4 * (f // 2 + 1) + (2 if step == 0 else 4), 4 * B))
                split_mm(up_banks(m)[0], 0, e, x1T_hi[:, f % 2], x1T_lo[:, f % 2]).then_inc(h1_ready, 1)
                split_mm(up_banks(m)[1], 1, e, x1T_hi[:, f % 2], x1T_lo[:, f % 2]).then_inc(h3_ready, 1)

            def expert_down(m):
                f, e = m // NE, expert(m)
                to, first, last = ps_y[f % 2][:, :], m % NE == 0, m % NE == NE - 1 or m % STEPS == DIRECT[0] - 1
                if first:
                    pe.wait_ge(w_lo_ready, 3)
                    if f % 2:
                        pe.wait_ge(gatesT_ready, f + 1)
                    else:
                        pe.wait_ge(y1_ready, CT * (f + 2))
                pe.wait_ge(h_lo_ready, split(m + 1))
                split_mm(to, 2, e, h_hi[:, m % SLOTS], h_lo[:, m % SLOTS], start=first, stop=last
                         ).then_inc(h_used, 1)

            def transpose_y(f):
                pe.wait_ge(yT_ready, f + 1)
                transpose4(ps_z[:, :], lambda t: yT[:, 0, P * t:P * (t + 1)]).then_inc(y_made, 1)

            def finish_y(f):
                m0 = NE * (f + 1) - len(DIRECT)
                for k in range(2):
                    pe.wait_ge(h_ready, m0 + k + 1)
                    if f == NCH - 1:
                        t0 = CT * f + CT // 2 * k
                        mm(ps_half[k], ident[:, :], x1[:, t0:t0 + CT // 2, :].rearrange("p t d -> p (t d)"),
                           start=True, stop=False)
                    else:
                        mm(ps_half[k], warm[:, 0:P], warm[:, 0:C // 2], start=True, stop=False)
                    for m in (m0, m0 + 1):
                        pe.wait_ge(h_ready, m + 1)
                        e = expert(m)
                        for t in range(CT // 2):
                            q = P * (CT // 2 * k + t)
                            mm(ps_half[k][:, P * t:P * (t + 1)], h[:, m % H_SLOTS, q:q + P],
                               wf[2][:, P * e:P * (e + 1)], start=False, stop=False)
                    pe.wait_ge(yT_ready, f + 1)
                    for t in range(CT // 2):
                        q = P * (CT // 2 * k + t)
                        last = mm(ps_half[k][:, P * t:P * (t + 1)], yT[:, 1, q:q + P], ident[:, :],
                                  start=False, stop=t == CT // 2 - 1)
                    last.then_inc(y_half_made, 1)

            pe.wait_ge(warm_ready, 1)
            for _ in range(WARM):
                mm(ps_m[:, :], warm[:, 0:P], warm[:, :], start=True, stop=True)
            pe.wait_ge(watt_ready, 1)
            project(0, 0)
            project(0, 1)
            project(0, 4)
            pe.wait_ge(consts_ready, 3)
            scores(0, 0)
            scores(0, 1)
            for b in range(B):
                f = 2 * b
                for i in range(ST):
                    if 0 and i:
                        attend(b, i - 1)
                    if 1 <= i < ST - 1:
                        scores(b, i + 1)
                    if b == 0 and i < 3:
                        project(0, (2, 3, 5)[i])
                    if b:
                        for k in range(DEFERRED[i] if i < len(DEFERRED) else 0):
                            expert_down(down)
                            down += 1
                        if i == 2:
                            finish_y(f - 1)
                    if not 0 and i:
                        attend(b, i - 1)
                    if 0 and i == 6:
                        transpose_x1(f)
                    if 1 and i == 7:
                        logits_T(f)
                    if 0 and i == 7:
                        transpose_logits(f)
                    transpose_probs(b, i)
                    if not 0 and i == 6:
                        transpose_x1(f)
                    if not 1 and i == 7:
                        logits_T(f)
                    if not 0 and i == 7:
                        transpose_logits(f)
                    if b + 1 < B and i == 6:
                        project(b + 1, 0)
                        project(b + 1, 1)
                if b + 1 < B and 1 < 0:
                    project(b + 1, 2)
                    project(b + 1, 3)
                if -2 == 0:
                    transpose_gates(f)
                attend(b, ST - 1)
                if 8 == 7:
                    transpose_logits(f)
                if -1 == 0:
                    transpose_gates(f)
                down = NE * f
                for step in range(STEPS):
                    if b + 1 < B and step == 1:
                        project(b + 1, 2)
                        project(b + 1, 3)
                    expert_up(NE * f + step)
                    for _ in range(DOWNS[step]):
                        expert_down(down)
                        down += 1
                    if step == 0:
                        transpose_gates(f)
                    if step == 1:
                        transpose_x1(f + 1)
                    if step == 3:
                        logits_T(f + 1)
                    if step == 4:
                        transpose_logits(f + 1)
                    if step == 7:
                        transpose_gates(f + 1)
                    if step == 14:
                        transpose_y(f)
                if b + 1 < B:
                    project(b + 1, 4)
                    project(b + 1, 5)
                    scores(b + 1, 0)
                    scores(b + 1, 1)
                else:
                    for m in range(down, NE * f + STEPS - len(DIRECT)):
                        expert_down(m)
            finish_y(NCH - 1)


def kernel(L0_attn_x, L0_attn_Wq, L0_attn_bq, L0_attn_Wk, L0_attn_bk, L0_attn_Wv, L0_attn_bv, L0_ffn_gate_w,
           L0_ffn_gate_bias, L0_ffn_w1, L0_ffn_w3, L0_ffn_w2, L0_ffn_sw1, L0_ffn_sw3, L0_ffn_sw2):
    import numpy as np
    import concourse.bacc as bacc
    from concourse import mybir as mb
    from concourse.bass_utils import run_bass_kernel_spmd

    x = np.asarray(L0_attn_x)
    B, S, D = x.shape
    up = lambda shared, routed: np.concatenate(
        [np.asarray(shared), np.asarray(routed).reshape(-1, D)], axis=0).T
    down = np.concatenate(
        [np.asarray(L0_ffn_sw2).reshape(D, -1, D).transpose(2, 1, 0), np.asarray(L0_ffn_w2).transpose(2, 0, 1)],
        axis=1).reshape(D, -1)
    ins = {
        "x": x,
        "xT": x.reshape(B * S, D).T,
        "w_att": np.concatenate([np.asarray(w).T for w in (L0_attn_Wk, L0_attn_Wq, L0_attn_Wv)], axis=1),
        "cols": np.stack([np.asarray(L0_attn_bq), np.asarray(L0_attn_bk), *np.asarray(L0_ffn_gate_w)], axis=1),
        "rows": np.concatenate([np.asarray(L0_attn_bv), np.asarray(L0_ffn_gate_bias)]),
        "w1T": up(L0_ffn_sw1, L0_ffn_w1),
        "w3T": up(L0_ffn_sw3, L0_ffn_w3),
        "w2T": down,
    }
    nc = bacc.Bacc("TRN2", target_bir_lowering=False, num_devices=1)
    arrays, args = {}, []
    for name, a in ins.items():
        a = np.ascontiguousarray(a)
        arrays[f"in_{name}_dram"] = a
        args.append(nc.dram_tensor(f"in_{name}_dram", a.shape, mb.dt.from_np(a.dtype), kind="ExternalInput").ap())
    args.append(nc.dram_tensor("out_0_dram", (B, S, D), mb.dt.from_np(x.dtype), kind="ExternalOutput").ap())
    attention_moe_block(nc, *args)
    r = run_bass_kernel_spmd(nc, [arrays], core_ids=[0])
    return r.results[0]["out_0_dram"]
```

```python
import concourse.bass as bass
from concourse import mybir
from contextlib import ExitStack


def attention_moe_block(nc, x, xT_in, w_att, cols_in, rows_in, w1T_in, w3T_in, w2T_in, out):
    f32, f32r, bf16 = mybir.dt.float32, mybir.dt.float32r, mybir.dt.bfloat16
    u32, i32 = mybir.dt.uint32, mybir.dt.int32
    ALU, ACT, AX = mybir.AluOpType, mybir.ActivationFunctionType, mybir.AxisListType

    B, S, D = x.shape
    P = 128
    C = 512
    CT = C // P
    ST = S // P
    NCH = B * S // C
    E = cols_in.shape[1] - 2
    NE = w1T_in.shape[1] // P
    SH = NE - E
    SCALE = float(D) ** -0.5
    EPS = 1e-5
    MASKED = -1e30
    WARM = 9
    FIRST = 2
    SLOTS = 4
    H_SLOTS = 8
    UPS = 3
    STEPS = 2 * NE
    DIRECT = (STEPS - 2, STEPS - 1)
    HIGHS = [[], [0], [1], [2], [], [3], [], [4], [], [5, 6, 7], [], [8], [9, 10, 11],
             [12], [], [], [13, 14, 15], [16], [17], []]
    DOWNS = [0, 0, 1, 0, 1, 0, 1, 0, 0, 1, 0, 0, 5, 2, 0, 1, 0, 1, 0, 3]
    DEFERRED = [2, 0, 0]
    assert D == P and S == 2 * C and B == 2

    GROUPS = [[(j0, min(j0 + CT, i + 1)) for j0 in range(0, i + 1, CT)] for i in range(ST)]
    G0 = [sum(len(g) for g in GROUPS[:i]) for i in range(ST + 1)]
    GPS = G0[ST]

    BY_ACT = [0, 1, 1, 1, 0, 1, 1, 1, 0, 1, 0, 1]

    def by_act(g):
        return BY_ACT[g % GPS] == 1

    def groups_of(act, upto):
        return sum(by_act(g % GPS) == act for g in range(upto))

    gates_dram = nc.dram_tensor("gates_scratch", (NCH, E * CT, P), f32, kind="Internal").ap()

    with ExitStack() as ctx:
        def sb(name, shape, dt=f32):
            return ctx.enter_context(nc.sbuf_tensor(name, shape, dt))

        def sem(name):
            return ctx.enter_context(nc.semaphore(name))

        ident = sb("ident", [P, P])
        ident16 = sb("ident16", [P, P], bf16)
        mask16 = sb("mask16", [P, P], bf16)
        expert_no = sb("expert_no", [P, CT, E], i32)
        minus_half = sb("minus_half", [P, CT])
        watt = sb("watt", [P, 3 * P])
        cols = sb("cols", [P, 2 + E])
        bqk, gw = cols[:, 0:2], cols[:, 2:2 + E]
        rows = sb("rows", [P, D + E])
        bv, gb = rows[:, 0:D], rows[:, D:D + E]
        gw_hi = sb("gw_hi", [P, P], f32r)
        gw_lo = sb("gw_lo", [P, P], f32r)
        wf = [sb(f"w{n}", [P, NE * P]) for n in "132"]
        wf_hi = [sb(f"w{n}_hi", [P, NE * P], f32r) for n in "132"]
        wf_lo = [sb(f"w{n}_lo", [P, NE * P], f32r) for n in "132"]
        xs = sb("xs", [P, B * ST, D])
        xT = sb("xT", [P, B * S])
        kT = sb("kT", [P, S])
        qT = sb("qT", [P, S])
        kT_hi, kT_lo = sb("kT_hi", [P, S], f32r), sb("kT_lo", [P, S], f32r)
        qT_hi, qT_lo = sb("qT_hi", [P, S], f32r), sb("qT_lo", [P, S], f32r)
        v = sb("v", [P, ST, D])
        negmax = sb("negmax", [P, B * ST])
        rowsum = sb("rowsum", [P, B * ST])
        rinv = sb("rinv", [P, B * ST])
        probs = sb("probs", [P, 2, S])
        act_slots = sb("act_slots", [P, SLOTS + H_SLOTS, C])
        pT = act_slots[:, 0:4].rearrange("p (s k) c -> p s (k c)", s=2)
        silu, h = act_slots[:, 0:SLOTS], act_slots[:, SLOTS:SLOTS + H_SLOTS]
        y1 = xs
        x1 = sb("x1", [P, B * ST, D])
        x1T_hi = sb("x1T_hi", [P, 2, C], f32r)
        x1T_lo = sb("x1T_lo", [P, 2, C], f32r)
        stats = sb("stats", [P, B * ST, 6])
        mv1 = sb("mv1", [P, B * ST, 2])
        mv2 = sb("mv2", [P, B * ST, 2])
        ve1 = sb("ve1", [P, B * ST])
        ve2 = sb("ve2", [P, B * ST])
        rstd1 = sb("rstd1", [P, B * ST])
        rstd2 = sb("rstd2", [P, B * ST])
        logitsT = sb("logitsT", [E, C])
        lmax = sb("lmax", [P, CT])
        cent = sb("cent", [P, NCH, CT, E])
        expo = sb("expo", [P, NCH, CT, E])
        esum = sb("esum", [P, CT])
        einv = sb("einv", [P, CT])
        score = sb("score", [P, CT, E])
        biased = sb("biased", [P, CT, E])
        top = sb("top", [P, CT, 8])
        topi = sb("topi", [P, CT, 8], u32)
        is0 = sb("is0", [P, CT, E])
        is1 = sb("is1", [P, CT, E])
        gates = sb("gates", [P, NCH, P])
        gatesT = sb("gatesT", [P, NCH, P])
        gspread = sb("gspread", [P, 2, E, C])
        h_hi = sb("h_hi", [P, SLOTS, C], f32r)
        h_lo = sb("h_lo", [P, SLOTS, C], f32r)
        warm = sb("warm", [P, C], bf16)
        first_exp = sb("first_exp", [P, 1])
        yT = sb("yT", [P, 2, C])
        y2 = y1
        o = y2

        ps_s = ctx.enter_context(nc.psum_tensor("ps_s", [P, 2, S], f32))
        ps_t = ctx.enter_context(nc.psum_tensor("ps_t", [P, 2, C], f32))
        ps_z = ctx.enter_context(nc.psum_tensor("ps_z", [P, C], f32))
        ps_m = ctx.enter_context(nc.psum_tensor("ps_m", [P, C], f32))
        ps_y = [ps_z, ps_m]
        ps_half = [ps_s[:, k, C:C + C // 2] for k in range(2)]

        consts_ready, zeros_ready, warm_ready = sem("consts_ready"), sem("zeros_ready"), sem("warm_ready")
        pool_step = sem("pool_step")
        ld_xT = [sem(f"ld_xT{k}") for k in range(3)]
        ld_watt, ld_cols, ld_rows, ld_x = sem("ld_watt"), sem("ld_cols"), sem("ld_rows"), sem("ld_x")
        ld_wf = [sem(f"ld_w{n}") for n in "132"]
        watt_ready, w_hi_ready, w_lo_ready = sem("watt_ready"), sem("w_hi_ready"), sem("w_lo_ready")
        kq_made, kq_ready, v_made, v_ready = sem("kq_made"), sem("kq_ready"), sem("v_made"), sem("v_ready")
        scores_ready, negmax_ready, probs_ready = sem("scores_ready"), sem("negmax_ready"), sem("probs_ready")
        kq_hi_ready, kq_lo_ready = sem("kq_hi_ready"), sem("kq_lo_ready")
        pT_made, pT_by_act, pT_by_dve = sem("pT_made"), sem("pT_by_act"), sem("pT_by_dve")
        z_made, rinv_ready, y1_ready = sem("z_made"), sem("rinv_ready"), sem("y1_ready")
        stats1_ready, mv1_ready = sem("stats1_ready"), sem("mv1_ready")
        var1_ready, rstd1_ready, x1_ready = sem("var1_ready"), sem("rstd1_ready"), sem("x1_ready")
        x1T_made, x1T_hi_ready, x1T_lo_ready = sem("x1T_made"), sem("x1T_hi_ready"), sem("x1T_lo_ready")
        logitsT_made, logitsT_ready, logits_ready = sem("logitsT_made"), sem("logitsT_ready"), sem("logits_ready")
        cent_ready, expo_ready = sem("cent_ready"), sem("expo_ready")
        gates_ready, gatesT_made, gatesT_ready = sem("gates_ready"), sem("gatesT_made"), sem("gatesT_ready")
        gates_stored = sem("gates_stored")
        gates_spread = [[sem(f"gates_spread{k}{n}") for n in range(2)] for k in range(2)]
        h1_ready, h3_ready, silu_ready = sem("h1_ready"), sem("h3_ready"), sem("silu_ready")
        gated_ready = sem("gated_ready")
        h_ready, h_hi_ready, h_lo_ready, h_used = sem("h_ready"), sem("h_hi_ready"), sem("h_lo_ready"), sem("h_used")
        yT_ready, y_made, y_half_made = sem("yT_ready"), sem("y_made"), sem("y_half_made")
        y2_ready = sem("y2_ready")
        var2_ready, rstd2_ready, o_ready, stored = sem("var2_ready"), sem("rstd2_ready"), sem("o_ready"), sem("stored")
        dve_step = sem("dve_step")

        def split(upto):
            return sum(m % STEPS not in DIRECT for m in range(upto))

        def expert(m):
            f, k = divmod(m, NE)
            return (k + SH) % NE if f % 2 else k

        def gated(upto):
            return sum(expert(m) >= SH for m in range(upto))

        def up_banks(m):
            k = m % STEPS % UPS
            return (ps_t[:, 0, :], ps_t[:, 1, :]) if k == 2 else (ps_s[:, k, 0:C], ps_s[:, k, C:2 * C])

        def proj_bank(b, n):
            if b == 0:
                return [ps_s[:, 0, 0:C], ps_s[:, 0, C:2 * C], ps_z[:, :], ps_m[:, :], ps_t[:, 0, :], ps_m[:, :]][n]
            return ps_s[:, 0, C * n:C * (n + 1)] if n < 2 else ps_t[:, n % 2, :]

        block = ctx.enter_context(nc.Block())

        @block.sync
        def _(sp):
            sp.dma_start(xT[:, 0:C], xT_in[:, 0:C]).then_inc(ld_xT[0], 16)
            sp.dma_start(xT[:, C:S], xT_in[:, C:S]).then_inc(ld_xT[1], 16)
            for n in range(3):
                sp.dma_start(wf[n][:, :], (w1T_in, w3T_in, w2T_in)[n]).then_inc(ld_wf[n], 16)
            sp.dma_start(xs[:, :, :], x.rearrange("b (t p) d -> p (b t) d", p=P)).then_inc(ld_x, 16)
            sp.dma_start(xT[:, S:2 * S], xT_in[:, S:2 * S]).then_inc(ld_xT[2], 16)

            def spread_gates(f):
                sp.wait_ge(gatesT_ready, f + 1)
                sp.dma_start(gates_dram[f], gatesT[0:CT * E, f, :]).then_inc(gates_stored, 16)
                sp.wait_ge(gates_stored, 16 * (f + 1))
                if f >= 2:
                    sp.wait_ge(gated_ready, E * (f - 1))
                g = gates_dram[f].rearrange("(e t) q -> e (t q)", t=CT)
                for n, (e0, e1) in enumerate(((0, FIRST), (FIRST, E))):
                    sp.dma_start(gspread[:, f % 2, e0:e1, :], g[e0:e1].partition_broadcast(P)
                                 ).then_inc(gates_spread[f % 2][n], 16)

            def store(f, part=0, parts=1):
                sp.wait_ge(o_ready, f + part + 1)
                t0, t1 = CT * f + CT // parts * part, CT * f + CT // parts * (part + 1)
                sp.dma_start(out.rearrange("b (t p) d -> p (b t) d", p=P)[:, t0:t1, :], o[:, t0:t1, :]
                             ).then_inc(stored, 16)

            for b in range(B):
                spread_gates(2 * b)
                spread_gates(2 * b + 1)
                store(2 * b)
                if b + 1 < B:
                    store(2 * b + 1)
            store(NCH - 1, 0, 2)
            store(NCH - 1, 1, 2)
            sp.wait_ge(stored, 16 * (NCH + 1))

        @block.gpsimd
        def _(pool):
            steps = [0]

            def link(ins):
                steps[0] += 1
                ins.then_inc(pool_step, 1)
                pool.wait_ge(pool_step, steps[0])

            link(nc.gpsimd.memset(ident[:, :], 0.0))
            nc.gpsimd.affine_select(out=ident[:, :], in_=ident[:, :], compare_op=ALU.not_equal, fill=1.0,
                                    base=0, pattern=[[-1, P]], channel_multiplier=1).then_inc(consts_ready, 1)
            link(nc.gpsimd.memset(ident16[:, :], 0.0))
            nc.gpsimd.affine_select(out=ident16[:, :], in_=ident16[:, :], compare_op=ALU.not_equal, fill=1.0,
                                    base=0, pattern=[[-1, P]], channel_multiplier=1).then_inc(consts_ready, 1)
            link(nc.gpsimd.memset(mask16[:, :], 0.0))
            nc.gpsimd.affine_select(out=mask16[:, :], in_=mask16[:, :], compare_op=ALU.is_ge, fill=MASKED,
                                    base=0, pattern=[[-1, P]], channel_multiplier=1).then_inc(consts_ready, 1)
            nc.gpsimd.iota(expert_no[:, :, :], pattern=[[0, CT], [1, E]], base=0,
                           channel_multiplier=0).then_inc(consts_ready, 1)
            nc.gpsimd.memset(gates[:, :, :], 0.0).then_inc(zeros_ready, 1)
            nc.gpsimd.memset(gw_hi[:, :].bitcast(f32), 0.0).then_inc(zeros_ready, 1)
            nc.gpsimd.memset(gw_lo[:, :].bitcast(f32), 0.0).then_inc(zeros_ready, 1)
            link(nc.gpsimd.memset(minus_half[:, :], -0.5))

            def w_low(n):
                pool.wait_ge(w_hi_ready, n + 1)
                nc.gpsimd.tensor_tensor(wf_lo[n][:, :], wf[n][:, :], wf_hi[n][:, :].bitcast(f32),
                                        ALU.subtract).then_inc(w_lo_ready, 1)

            def rstd1_tile(g):
                pool.wait_ge(var1_ready, g + 1)
                nc.gpsimd.tensor_tensor(rstd1[:, g:g + 1], ve1[:, g:g + 1], minus_half[:, 0:1],
                                        ALU.pow).then_inc(rstd1_ready, 1)

            def rstd2_chunk(f):
                pool.wait_ge(var2_ready, f + 1)
                nc.gpsimd.tensor_tensor(rstd2[:, CT * f:CT * (f + 1)], ve2[:, CT * f:CT * (f + 1)],
                                        minus_half[:, :], ALU.pow).then_inc(rstd2_ready, 1)

            def gate(m):
                f, e = m // NE, expert(m)
                if e < SH:
                    return
                if e == SH:
                    pool.wait_ge(gates_spread[f % 2][0], 16 * (f // 2 + 1))
                if e == SH + FIRST:
                    pool.wait_ge(gates_spread[f % 2][1], 16 * (f // 2 + 1))
                pool.wait_ge(h_ready, m + 1)
                nc.gpsimd.tensor_tensor(h[:, m % H_SLOTS], h[:, m % H_SLOTS], gspread[:, f % 2, e - SH, :],
                                        ALU.mult).then_inc(gated_ready, 1)

            for b in range(B):
                f = 2 * b
                for i in range(ST):
                    if b == 0 and i < 3:
                        w_low(i)
                    if b and i == 3:
                        rstd2_chunk(f - 1)
                    rstd1_tile(ST * b + i)
                for step in range(STEPS):
                    gate(NE * f + step)
                    if step == 19:
                        rstd2_chunk(f)
            for k in range(2):
                pool.wait_ge(var2_ready, NCH + k)
                t0 = B * ST - CT + CT // 2 * k
                nc.gpsimd.tensor_tensor(rstd2[:, t0:t0 + CT // 2], ve2[:, t0:t0 + CT // 2],
                                        minus_half[:, 0:CT // 2], ALU.pow).then_inc(rstd2_ready, 1)

        @block.scalar
        def _(act):
            act.dma_start(watt[:, :], w_att).then_inc(ld_watt, 16)
            act.dma_start(cols[:, :], cols_in).then_inc(ld_cols, 16)
            act.dma_start(rows[:, :], rows_in.partition_broadcast(P)).then_inc(ld_rows, 16)

            def kq_out(b, n):
                c, q = n // 2, n % 2
                act.wait_ge(kq_made, 4 * b + n + 1)
                nc.scalar.activation((qT if q else kT)[:, C * c:C * (c + 1)], proj_bank(b, n), ACT.Identity,
                                     bias=bqk[:, 1 - q:2 - q]).then_inc(kq_ready, 1)

            def kq_high(b, n):
                c, q = n // 2, n % 2
                act.wait_ge(kq_ready, 4 * b + n + 1)
                nc.scalar.copy((qT_hi if q else kT_hi)[:, C * c:C * (c + 1)], (qT if q else kT)[:, C * c:C * (c + 1)]
                               ).then_inc(kq_hi_ready, 1)

            def exp(b, i):
                g = b * ST + i
                act.wait_ge(negmax_ready, g + 1)
                if g >= 2:
                    act.wait_ge(pT_made, GPS * ((g - 2) // ST) + G0[(g - 2) % ST + 1])
                w = (i + 1) * P
                nc.scalar.activation(probs[:, g % 2, 0:w], ps_s[:, g % 2, 0:w], ACT.Exp,
                                     bias=negmax[:, g:g + 1], accum_out=rowsum[:, g:g + 1]).then_inc(probs_ready, 1)

            def pT_out(b, i):
                for g, (j0, j1) in enumerate(GROUPS[i]):
                    n = G0[i] + g
                    if not by_act(n):
                        continue
                    act.wait_ge(pT_made, GPS * b + n + 1)
                    nc.scalar.copy(pT[:, i % 2, P * j0:P * j1], ps_t[:, n % 2, 0:P * (j1 - j0)]).then_inc(pT_by_act, 1)

            def x1T_high(f):
                act.wait_ge(x1T_made, f + 1)
                nc.scalar.copy(x1T_hi[:, f % 2], ps_m[:, :]).then_inc(x1T_hi_ready, 1)

            def logitsT_out(f):
                act.wait_ge(logitsT_made, f + 1)
                nc.scalar.copy(logitsT[:, :], ps_m[0:E, :]).then_inc(logitsT_ready, 1)

            def router_exp(f):
                act.wait_ge(cent_ready, f + 1)
                nc.scalar.activation(expo[:, f], cent[:, f], ACT.Exp).then_inc(expo_ready, 1)

            def gatesT_out(f):
                act.wait_ge(gatesT_made, f + 1)
                nc.scalar.copy(gatesT[:, f], ps_m[:, 0:P]).then_inc(gatesT_ready, 1)

            def yT_out(f):
                act.wait_ge(h_used, split(NE * (f + 1)))
                nc.scalar.copy(yT[:, f % 2], ps_y[f % 2][:, :]).then_inc(yT_ready, 1)

            def silu_step(m):
                act.wait_ge(h1_ready, m + 1)
                if m >= SLOTS:
                    act.wait_ge(h_ready, m - SLOTS + 1)
                nc.scalar.activation(silu[:, m % SLOTS], up_banks(m)[0], ACT.Silu).then_inc(silu_ready, 1)

            def h_high(m):
                if m % STEPS in DIRECT:
                    return
                if expert(m) < SH:
                    act.wait_ge(h_ready, m + 1)
                else:
                    act.wait_ge(gated_ready, gated(m + 1))
                if m >= SLOTS:
                    act.wait_ge(h_used, split(m - SLOTS + 1))
                nc.scalar.copy(h_hi[:, m % SLOTS], h[:, m % H_SLOTS]).then_inc(h_hi_ready, 1)

            act.wait_ge(warm_ready, 1)
            nc.scalar.activation(first_exp[:, :], warm[:, 0:1], ACT.Exp)
            act.wait_ge(ld_cols, 16)
            act.wait_ge(watt_ready, 2)
            kq_out(0, 0)
            kq_out(0, 1)
            for b in range(B):
                f = 2 * b
                exp(b, 0)
                for i in range(ST):
                    if i + 1 < ST:
                        exp(b, i + 1)
                    if b == 0 and i < 2:
                        kq_out(0, 2 + i)
                    if b and i == 0:
                        yT_out(f - 1)
                    if i == ST - 1:
                        logitsT_out(f)
                    pT_out(b, i)
                    if i == ST - 2:
                        x1T_high(f)
                    if b + 1 < B and i == ST - 2:
                        kq_out(b + 1, 0)
                        kq_out(b + 1, 1)
                    if i == ST - 1:
                        router_exp(f)
                for step in range(STEPS):
                    if step == 1:
                        gatesT_out(f)
                    if step == 2:
                        x1T_high(f + 1)
                    if step == 3:
                        logitsT_out(f + 1)
                    if step == 5:
                        router_exp(f + 1)
                    if b + 1 < B and step == 1:
                        kq_out(b + 1, 2)
                        kq_out(b + 1, 3)
                    silu_step(NE * f + step)
                    if b + 1 < B and 6 <= step < 10:
                        kq_high(b + 1, step - 6)
                    if step == 13:
                        yT_out(f)
                    if step == 8:
                        gatesT_out(f + 1)
                    for k in HIGHS[step]:
                        h_high(NE * f + k)
            yT_out(NCH - 1)

        @block.vector
        def _(dve):
            steps = [0]

            def written(ins):
                steps[0] += 1
                ins.then_inc(dve_step, 1)

            def link(ins):
                written(ins)
                dve.wait_ge(dve_step, steps[0])

            def row_max(b, i):
                g = b * ST + i
                dve.wait_ge(scores_ready, g + 1)
                nc.vector.tensor_reduce(negmax[:, g:g + 1], ps_s[:, g % 2, 0:(i + 1) * P], AX.X, ALU.max,
                                        negate=True).then_inc(negmax_ready, 1)

            def pT_out(b, i):
                for g, (j0, j1) in enumerate(GROUPS[i]):
                    n = G0[i] + g
                    if by_act(n):
                        continue
                    dve.wait_ge(pT_made, GPS * b + n + 1)
                    nc.vector.tensor_copy(pT[:, i % 2, P * j0:P * j1], ps_t[:, n % 2, 0:P * (j1 - j0)]
                                          ).then_inc(pT_by_dve, 1)

            def kq_low(b, n):
                c, q = n // 2, n % 2
                dve.wait_ge(kq_hi_ready, 4 * (b - 1) + n + 1)
                full, hi, lo = (qT, qT_hi, qT_lo) if q else (kT, kT_hi, kT_lo)
                nc.vector.tensor_tensor(lo[:, C * c:C * (c + 1)], full[:, C * c:C * (c + 1)],
                                        hi[:, C * c:C * (c + 1)].bitcast(f32), ALU.subtract).then_inc(kq_lo_ready, 1)

            def v_out(b, n):
                dve.wait_ge(v_made, 2 * b + n + 1)
                nc.vector.tensor_tensor(v[:, CT * n:CT * (n + 1), :],
                                        proj_bank(b, 4 + n).rearrange("p (t d) -> p t d", d=D),
                                        bv.unsqueeze(1).to_broadcast([P, CT, D]), ALU.add).then_inc(v_ready, 1)

            def norm1_sum(g):
                dve.wait_ge(z_made, g + 1)
                if g == 0:
                    dve.wait_ge(ld_x, 16)
                dve.wait_ge(rinv_ready, g + 1)
                t = g % CT
                nc.vector.scalar_tensor_tensor(y1[:, g, :], ps_z[:, P * t:P * (t + 1)], rinv[:, g:g + 1],
                                               xs[:, g, :], ALU.mult, ALU.add).then_inc(y1_ready, 1)

            def norm1_rinv(g):
                dve.wait_ge(probs_ready, g + 1)
                nc.vector.reciprocal(rinv[:, g:g + 1], rowsum[:, g:g + 1]).then_inc(rinv_ready, 1)

            def norm1_stats(g):
                dve.wait_ge(y1_ready, g + 1)
                nc.vector.bn_stats(stats[:, g, :], y1[:, g, :]).then_inc(stats1_ready, 1)

            def norm1_mean(g):
                dve.wait_ge(stats1_ready, g + 1)
                nc.vector.bn_aggr(mv1[:, g, :], stats[:, g, :]).then_inc(mv1_ready, 1)

            def norm1_var(g):
                dve.wait_ge(mv1_ready, g + 1)
                nc.vector.tensor_scalar(ve1[:, g:g + 1], mv1[:, g, 1:2], EPS, None, ALU.add).then_inc(var1_ready, 1)

            def norm1_apply(g):
                dve.wait_ge(rstd1_ready, g + 1)
                nc.vector.tensor_scalar(x1[:, g, :], y1[:, g, :], mv1[:, g, 0:1], rstd1[:, g:g + 1],
                                        ALU.subtract, ALU.mult).then_inc(x1_ready, 1)

            def x1T_low(f):
                dve.wait_ge(x1T_hi_ready, f + 1)
                nc.vector.tensor_tensor(x1T_lo[:, f % 2], ps_m[:, :], x1T_hi[:, f % 2].bitcast(f32),
                                        ALU.subtract).then_inc(x1T_lo_ready, 1)

            def router_centre(f):
                dve.wait_ge(logits_ready, f + 1)
                lg = ps_m[:, 0:CT * E].rearrange("p (t e) -> p t e", e=E)
                link(nc.vector.tensor_reduce(lmax[:, :], lg, AX.X, ALU.max))
                nc.vector.tensor_tensor(cent[:, f], lg, lmax[:, :].unsqueeze(2).to_broadcast([P, CT, E]),
                                        ALU.subtract).then_inc(cent_ready, 1)

            def router_scores(f):
                dve.wait_ge(consts_ready, 4)
                dve.wait_ge(expo_ready, f + 1)
                link(nc.vector.tensor_reduce(esum[:, :], expo[:, f], AX.X, ALU.add))
                link(nc.vector.reciprocal(einv[:, :], esum[:, :]))
                link(nc.vector.tensor_tensor(score[:, :, :], expo[:, f],
                                             einv[:, :].unsqueeze(2).to_broadcast([P, CT, E]), ALU.mult))
                written(nc.vector.tensor_tensor(biased[:, :, :], score[:, :, :],
                                                gb.unsqueeze(1).to_broadcast([P, CT, E]), ALU.add))

            def router_top(f):
                dve.wait_ge(dve_step, steps[0])
                for t in range(CT):
                    last = nc.vector.max(top[:, t, :], biased[:, t, :])
                link(last)
                for t in range(CT):
                    last = nc.vector.max_index(topi[:, t, :], top[:, t, :], biased[:, t, :])
                written(last)

            def router_gates(f):
                dve.wait_ge(dve_step, steps[0])
                nc.vector.tensor_tensor(is0[:, :, :], expert_no[:, :, :],
                                        topi[:, :, 0:1].to_broadcast([P, CT, E]), ALU.is_equal)
                link(nc.vector.tensor_tensor(is1[:, :, :], expert_no[:, :, :],
                                             topi[:, :, 1:2].to_broadcast([P, CT, E]), ALU.is_equal))
                link(nc.vector.tensor_tensor(is0[:, :, :], is0[:, :, :], is1[:, :, :], ALU.add))
                nc.vector.tensor_tensor(gates[:, f, 0:CT * E].rearrange("p (e t) -> p t e", t=CT),
                                        score[:, :, :], is0[:, :, :], ALU.mult).then_inc(gates_ready, 1)

            def h_step(m):
                dve.wait_ge(silu_ready, m + 1)
                dve.wait_ge(h3_ready, m + 1)
                if m >= H_SLOTS:
                    dve.wait_ge(h_hi_ready, split(m - H_SLOTS + 1))
                    if (m - H_SLOTS) % STEPS in DIRECT:
                        dve.wait_ge(y_half_made, 2 * (m // STEPS))
                nc.vector.tensor_tensor(h[:, m % H_SLOTS], silu[:, m % SLOTS], up_banks(m)[1],
                                        ALU.mult).then_inc(h_ready, 1)

            def h_low(m):
                if m % STEPS in DIRECT:
                    return
                dve.wait_ge(h_hi_ready, split(m + 1))
                nc.vector.tensor_tensor(h_lo[:, m % SLOTS], h[:, m % H_SLOTS], h_hi[:, m % SLOTS].bitcast(f32),
                                        ALU.subtract).then_inc(h_lo_ready, 1)

            def norm2_sum_half(f, k):
                dve.wait_ge(y_half_made, f + k)
                t0 = CT * f + CT // 2 * k
                nc.vector.tensor_tensor(y2[:, t0:t0 + CT // 2, :], ps_half[k].rearrange("p (t d) -> p t d", d=D),
                                        x1[:, t0:t0 + CT // 2, :], ALU.add).then_inc(y2_ready, 1)

            def norm2_sum(f):
                dve.wait_ge(y_made, f // 2 + 1)
                nc.vector.tensor_tensor(y2[:, CT * f:CT * (f + 1), :], ps_z[:, :].rearrange("p (t d) -> p t d", d=D),
                                        x1[:, CT * f:CT * (f + 1), :], ALU.add).then_inc(y2_ready, 2)

            def norm2_stats(f, k=0, parts=1):
                t0, t1 = CT * f + CT // parts * k, CT * f + CT // parts * (k + 1)
                dve.wait_ge(y2_ready, 2 * f + 2 * (k + 1) // parts)
                for g in range(t0, t1):
                    last = nc.vector.bn_stats(stats[:, g, :], y2[:, g, :])
                link(last)
                for g in range(t0, t1):
                    last = nc.vector.bn_aggr(mv2[:, g, :], stats[:, g, :])
                link(last)
                nc.vector.tensor_scalar(ve2[:, t0:t1], mv2[:, t0:t1, 1], EPS, None, ALU.add).then_inc(var2_ready, 1)

            def norm2_apply(f, k=0, parts=1):
                dve.wait_ge(rstd2_ready, f + k + 1)
                for g in range(CT * f + CT // parts * k, CT * f + CT // parts * (k + 1)):
                    last = nc.vector.tensor_scalar(o[:, g, :], y2[:, g, :], mv2[:, g, 0:1], rstd2[:, g:g + 1],
                                                   ALU.subtract, ALU.mult)
                last.then_inc(o_ready, 1)

            def w_high(n):
                dve.wait_ge(ld_wf[n], 16)
                nc.vector.tensor_copy(wf_hi[n][:, :], wf[n][:, :]).then_inc(w_hi_ready, 1)

            nc.vector.memset(warm[:, :], 0.0).then_inc(warm_ready, 1)
            dve.wait_ge(ld_watt, 16)
            nc.vector.tensor_scalar(watt[:, P:2 * P], watt[:, P:2 * P], SCALE, None, ALU.mult).then_inc(watt_ready, 1)
            dve.wait_ge(ld_cols, 16)
            nc.vector.tensor_scalar(bqk[:, 0:1], bqk[:, 0:1], SCALE, None, ALU.mult).then_inc(watt_ready, 1)
            dve.wait_ge(zeros_ready, 3)
            link(nc.vector.tensor_copy(gw_hi[:, 0:E], gw))
            nc.vector.tensor_tensor(gw_lo[:, 0:E], gw, gw_hi[:, 0:E].bitcast(f32), ALU.subtract)
            for b in range(B):
                f = 2 * b
                row_max(b, 0)
                if b == 0:
                    dve.wait_ge(ld_rows, 16)
                    v_out(0, 0)
                for i in range(ST):
                    g = ST * b + i
                    if i + 1 < ST:
                        row_max(b, i + 1)
                    if b and i == 2:
                        norm2_sum_half(f - 1, 0)
                        norm2_sum_half(f - 1, 1)
                    norm1_rinv(g)
                    if b == 0 and i == 2:
                        v_out(0, 1)
                    if i >= 2:
                        norm1_mean(g - 2)
                    if i >= 1:
                        norm1_sum(g - 1)
                    if i >= 2:
                        norm1_var(g - 2)
                    if i >= 3:
                        norm1_apply(g - 3)
                    pT_out(b, i)
                    if i >= 1:
                        norm1_stats(g - 1)
                    if b == 0 and i < 3:
                        w_high(i)
                    if i == ST - 2:
                        x1T_low(f)
                    if b and i == 3:
                        norm2_stats(f - 1)
                    if b and i == 5:
                        norm2_apply(f - 1)
                router_centre(f)
                norm1_mean(g - 1)
                router_scores(f)
                router_top(f)
                norm1_var(g - 1)
                router_gates(f)
                norm1_sum(g)
                norm1_stats(g)
                norm1_mean(g)
                norm1_var(g)
                norm1_apply(g - 2)
                norm1_apply(g - 1)
                norm1_apply(g)
                for step in range(STEPS):
                    m = NE * f + step
                    if step == 2:
                        x1T_low(f + 1)
                    if step == 4:
                        router_centre(f + 1)
                    if step == 5:
                        router_scores(f + 1)
                        router_top(f + 1)
                        router_gates(f + 1)
                    h_step(m)
                    if b + 1 < B and 7 <= step < 11:
                        kq_low(b + 1, step - 7)
                    for k in HIGHS[step]:
                        h_low(NE * f + k)
                    if step == 16:
                        norm2_sum(f)
                    elif step == 17:
                        norm2_stats(f)
                    elif step == 19:
                        norm2_apply(f)
                if b + 1 < B:
                    v_out(b + 1, 0)
                    v_out(b + 1, 1)
            for k in range(2):
                norm2_sum_half(NCH - 1, k)
                norm2_stats(NCH - 1, k, 2)
            for k in range(2):
                norm2_apply(NCH - 1, k, 2)

        @block.tensor
        def _(pe):
            mm = nc.tensor.matmul

            def project(b, n):
                if b:
                    pe.wait_ge(ld_xT[2], 16)
                    if n < 2:
                        pe.wait_ge(probs_ready, ST * b - 1)
                    elif n < 4:
                        pe.wait_ge(pT_by_act, groups_of(True, GPS * b))
                        pe.wait_ge(pT_by_dve, groups_of(False, GPS * b))
                    else:
                        pe.wait_ge(h_ready, STEPS * b - 2)
                else:
                    pe.wait_ge(ld_xT[1 if n in (2, 3, 5) else 0], 16)
                    if n == 5:
                        pe.wait_ge(kq_ready, 4)
                to = proj_bank(b, n)
                if n < 4:
                    c, q = n // 2, n % 2
                    mm(to, watt[:, P * q:P * (q + 1)], xT[:, S * b + C * c:S * b + C * (c + 1)],
                       start=True, stop=True).then_inc(kq_made, 1)
                else:
                    for t in range(CT):
                        tok = S * b + C * (n - 4) + P * t
                        last = mm(to[:, P * t:P * (t + 1)], xT[:, tok:tok + P], watt[:, 2 * P:3 * P],
                                  start=True, stop=True)
                    last.then_inc(v_made, 1)

            def scores(b, i):
                g = b * ST + i
                if i in (0, CT):
                    pe.wait_ge(kq_ready, 4 * b + (4 if i else 2))
                if g >= 2 and i >= 2:
                    pe.wait_ge(probs_ready, g - 1)
                if b and i < 2:
                    pe.wait_ge(h_ready, STEPS * b - 1 + i)
                if b and i in (CT, CT + 1):
                    pe.wait_ge(y2_ready, 4 * b - 1 + i - CT)
                q = qT[:, P * i:P * (i + 1)]
                for k0 in range(0, (i + 1) * P, C):
                    k1 = min(k0 + C, (i + 1) * P)
                    diagonal = k1 == (i + 1) * P
                    to = ps_s[:, g % 2, k0:k1]
                    if b == 0 or k1 - k0 < C:
                        mm(to, q, kT[:, k0:k1], start=True, stop=not diagonal)
                        continue
                    pe.wait_ge(kq_lo_ready, 4 * (b - 1) + (2 if i < CT else 4))
                    q_hi, q_lo = qT_hi[:, P * i:P * (i + 1)], qT_lo[:, P * i:P * (i + 1)]
                    mm(to, q_lo, kT_hi[:, k0:k1], start=True, stop=False)
                    mm(to, q_hi, kT_lo[:, k0:k1], start=False, stop=False)
                    mm(to, q_hi, kT_hi[:, k0:k1], start=False, stop=not diagonal)
                last = mm(ps_s[:, g % 2, P * i:P * (i + 1)], ident16[:, :], mask16[:, :], start=False, stop=True)
                last.then_inc(scores_ready, 1)

            def transpose_probs(b, i):
                g = b * ST + i
                pe.wait_ge(probs_ready, g + 1)
                for k, (j0, j1) in enumerate(GROUPS[i]):
                    n = G0[i] + k
                    if n < 2:
                        if b or n == 0:
                            pe.wait_ge(v_ready, 2 * b + n + 1)
                    else:
                        a = by_act(n - 2)
                        pe.wait_ge(pT_by_act if a else pT_by_dve, groups_of(a, GPS * b + n - 1))
                    for j in range(j0, j1):
                        last = nc.tensor.transpose(ps_t[:, n % 2, P * (j - j0):P * (j - j0 + 1)],
                                                   probs[:, g % 2, P * j:P * (j + 1)], ident[:, :])
                    last.then_inc(pT_made, 1)

            def attend(b, i):
                g = ST * b + i
                pe.wait_ge(pT_by_act, groups_of(True, GPS * b + G0[i + 1]))
                pe.wait_ge(pT_by_dve, groups_of(False, GPS * b + G0[i + 1]))
                if i in (0, CT):
                    pe.wait_ge(v_ready, 2 * b + 1 + i // CT)
                if g:
                    pe.wait_ge(y1_ready, g)
                else:
                    pe.wait_ge(kq_ready, 3)
                if b and i == 0:
                    pe.wait_ge(y2_ready, 4 * b - 2)
                t = i % CT
                for j in range(i + 1):
                    last = mm(ps_z[:, P * t:P * (t + 1)], pT[:, i % 2, P * j:P * (j + 1)], v[:, j, :],
                              start=j == 0, stop=j == i)
                last.then_inc(z_made, 1)

            def transpose4(to, src):
                for t in range(CT):
                    last = nc.tensor.transpose(to[:, P * t:P * (t + 1)], src(t), ident[:, :])
                return last

            def transpose_x1(f):
                pe.wait_ge(x1_ready, CT * (f + 1))
                if f % 2:
                    pe.wait_ge(gatesT_ready, f)
                transpose4(ps_m[:, :], lambda t: x1[:, CT * f + t, :]).then_inc(x1T_made, 1)

            def logits_T(f):
                pe.wait_ge(x1T_lo_ready, f + 1)
                hi, lo = x1T_hi[:, f % 2], x1T_lo[:, f % 2]
                mm(ps_m[:, :], gw_lo[:, :], hi, start=True, stop=False)
                mm(ps_m[:, :], gw_hi[:, :], lo, start=False, stop=False)
                mm(ps_m[:, :], gw_hi[:, :], hi, start=False, stop=True).then_inc(logitsT_made, 1)

            def transpose_logits(f):
                pe.wait_ge(logitsT_ready, f + 1)
                for t in range(CT):
                    last = nc.tensor.transpose(ps_m[:, E * t:E * (t + 1)], logitsT[:, P * t:P * (t + 1)],
                                               ident[0:E, 0:E])
                last.then_inc(logits_ready, 1)

            def transpose_gates(f):
                pe.wait_ge(gates_ready, f + 1)
                nc.tensor.transpose(ps_m[:, 0:P], gates[:, f, :], ident[:, :]).then_inc(gatesT_made, 1)

            def split_mm(to, n, e, hi, lo, start=True, stop=True):
                w_hi, w_lo = wf_hi[n][:, P * e:P * (e + 1)], wf_lo[n][:, P * e:P * (e + 1)]
                mm(to, w_lo, hi, start=start, stop=False)
                mm(to, w_hi, lo, start=False, stop=False)
                return mm(to, w_hi, hi, start=False, stop=stop)

            def expert_up(m):
                f, e = m // NE, expert(m)
                step = m % STEPS
                if m % NE == 0:
                    pe.wait_ge(x1T_lo_ready, f + 1)
                    pe.wait_ge(w_lo_ready, 2)
                if step >= UPS:
                    pe.wait_ge(h_ready, m - UPS + 1)
                elif step < 2:
                    pe.wait_ge(probs_ready, ST * (f // 2 + 1) - 1 + step)
                else:
                    pe.wait_ge(pT_by_act, groups_of(True, GPS * (f // 2 + 1)))
                    pe.wait_ge(pT_by_dve, groups_of(False, GPS * (f // 2 + 1)))
                if step in (0, 2):
                    pe.wait_ge(kq_ready, min(4 * (f // 2 + 1) + (2 if step == 0 else 4), 4 * B))
                split_mm(up_banks(m)[0], 0, e, x1T_hi[:, f % 2], x1T_lo[:, f % 2]).then_inc(h1_ready, 1)
                split_mm(up_banks(m)[1], 1, e, x1T_hi[:, f % 2], x1T_lo[:, f % 2]).then_inc(h3_ready, 1)

            def expert_down(m):
                f, e = m // NE, expert(m)
                to, first, last = ps_y[f % 2][:, :], m % NE == 0, m % NE == NE - 1 or m % STEPS == DIRECT[0] - 1
                if first:
                    pe.wait_ge(w_lo_ready, 3)
                    if f % 2:
                        pe.wait_ge(gatesT_ready, f + 1)
                    else:
                        pe.wait_ge(y1_ready, CT * (f + 2))
                pe.wait_ge(h_lo_ready, split(m + 1))
                split_mm(to, 2, e, h_hi[:, m % SLOTS], h_lo[:, m % SLOTS], start=first, stop=last
                         ).then_inc(h_used, 1)

            def transpose_y(f):
                pe.wait_ge(yT_ready, f + 1)
                transpose4(ps_z[:, :], lambda t: yT[:, 0, P * t:P * (t + 1)]).then_inc(y_made, 1)

            def finish_y(f):
                m0 = NE * (f + 1) - len(DIRECT)
                for k in range(2):
                    pe.wait_ge(h_ready, m0 + k + 1)
                    mm(ps_half[k], warm[:, 0:P], warm[:, 0:C // 2], start=True, stop=False)
                    for m in (m0, m0 + 1):
                        pe.wait_ge(h_ready, m + 1)
                        e = expert(m)
                        for t in range(CT // 2):
                            q = P * (CT // 2 * k + t)
                            mm(ps_half[k][:, P * t:P * (t + 1)], h[:, m % H_SLOTS, q:q + P],
                               wf[2][:, P * e:P * (e + 1)], start=False, stop=False)
                    pe.wait_ge(yT_ready, f + 1)
                    for t in range(CT // 2):
                        q = P * (CT // 2 * k + t)
                        last = mm(ps_half[k][:, P * t:P * (t + 1)], yT[:, 1, q:q + P], ident[:, :],
                                  start=False, stop=t == CT // 2 - 1)
                    last.then_inc(y_half_made, 1)

            pe.wait_ge(warm_ready, 1)
            for _ in range(WARM):
                mm(ps_m[:, :], warm[:, 0:P], warm[:, :], start=True, stop=True)
            pe.wait_ge(watt_ready, 1)
            project(0, 0)
            project(0, 1)
            project(0, 4)
            pe.wait_ge(consts_ready, 3)
            scores(0, 0)
            scores(0, 1)
            for b in range(B):
                f = 2 * b
                for i in range(ST):
                    if 1 <= i < ST - 1:
                        scores(b, i + 1)
                    if b == 0 and i < 3:
                        project(0, (2, 3, 5)[i])
                    if b:
                        for k in range(DEFERRED[i] if i < len(DEFERRED) else 0):
                            expert_down(down)
                            down += 1
                        if i == 2:
                            finish_y(f - 1)
                    if i:
                        attend(b, i - 1)
                    if i == ST - 1:
                        logits_T(f)
                    transpose_probs(b, i)
                    if i == ST - 2:
                        transpose_x1(f)
                    if i == ST - 1:
                        transpose_logits(f)
                    if b + 1 < B and i == ST - 2:
                        project(b + 1, 0)
                        project(b + 1, 1)
                attend(b, ST - 1)
                down = NE * f
                for step in range(STEPS):
                    if b + 1 < B and step == 1:
                        project(b + 1, 2)
                        project(b + 1, 3)
                    expert_up(NE * f + step)
                    for _ in range(DOWNS[step]):
                        expert_down(down)
                        down += 1
                    if step == 0:
                        transpose_gates(f)
                    if step == 1:
                        transpose_x1(f + 1)
                    if step == 2:
                        logits_T(f + 1)
                    if step == 4:
                        transpose_logits(f + 1)
                    if step == 7:
                        transpose_gates(f + 1)
                    if step == 16:
                        transpose_y(f)
                if b + 1 < B:
                    project(b + 1, 4)
                    project(b + 1, 5)
                    scores(b + 1, 0)
                    scores(b + 1, 1)
                else:
                    for m in range(down, NE * f + STEPS - len(DIRECT)):
                        expert_down(m)
            finish_y(NCH - 1)


def kernel(L0_attn_x, L0_attn_Wq, L0_attn_bq, L0_attn_Wk, L0_attn_bk, L0_attn_Wv, L0_attn_bv, L0_ffn_gate_w,
           L0_ffn_gate_bias, L0_ffn_w1, L0_ffn_w3, L0_ffn_w2, L0_ffn_sw1, L0_ffn_sw3, L0_ffn_sw2):
    import numpy as np
    import concourse.bacc as bacc
    from concourse import mybir as mb
    from concourse.bass_utils import run_bass_kernel_spmd

    x = np.asarray(L0_attn_x)
    B, S, D = x.shape
    up = lambda shared, routed: np.concatenate(
        [np.asarray(shared), np.asarray(routed).reshape(-1, D)], axis=0).T
    down = np.concatenate(
        [np.asarray(L0_ffn_sw2).reshape(D, -1, D).transpose(2, 1, 0), np.asarray(L0_ffn_w2).transpose(2, 0, 1)],
        axis=1).reshape(D, -1)
    ins = {
        "x": x,
        "xT": x.reshape(B * S, D).T,
        "w_att": np.concatenate([np.asarray(w).T for w in (L0_attn_Wk, L0_attn_Wq, L0_attn_Wv)], axis=1),
        "cols": np.stack([np.asarray(L0_attn_bq), np.asarray(L0_attn_bk), *np.asarray(L0_ffn_gate_w)], axis=1),
        "rows": np.concatenate([np.asarray(L0_attn_bv), np.asarray(L0_ffn_gate_bias)]),
        "w1T": up(L0_ffn_sw1, L0_ffn_w1),
        "w3T": up(L0_ffn_sw3, L0_ffn_w3),
        "w2T": down,
    }
    nc = bacc.Bacc("TRN2", target_bir_lowering=False, num_devices=1)
    arrays, args = {}, []
    for name, a in ins.items():
        a = np.ascontiguousarray(a)
        arrays[f"in_{name}_dram"] = a
        args.append(nc.dram_tensor(f"in_{name}_dram", a.shape, mb.dt.from_np(a.dtype), kind="ExternalInput").ap())
    args.append(nc.dram_tensor("out_0_dram", (B, S, D), mb.dt.from_np(x.dtype), kind="ExternalOutput").ap())
    attention_moe_block(nc, *args)
    r = run_bass_kernel_spmd(nc, [arrays], core_ids=[0])
    return r.results[0]["out_0_dram"]
```
